# Optimizing a Trainium2 kernel written in Bass

```python
import numpy as np
import jax
import jax.numpy as jnp

def _softmax(x, axis=-1):
    return jax.nn.softmax(x, axis=axis)

def _gelu(x):
    return jax.nn.gelu(x, approximate=True)

def _silu(x):
    return jax.nn.silu(x)

def _sigmoid(x):
    return jax.nn.sigmoid(x)

def _layernorm(x, axis=-1, eps=1e-05):
    m = jnp.mean(x, axis=axis, keepdims=True)
    v = jnp.var(x, axis=axis, keepdims=True)
    return (x - m) / jnp.sqrt(v + eps)

def _scatter_add(tgt, idx, src, axis=0):
    return tgt.at[idx].add(src)

def _segment_sum(src, seg, n):
    return jax.ops.segment_sum(src, seg, n)
kernel_name = 'mk_adj_ffn_d1_adj_r2_5cd2df'

def setup_inputs(seed: int=0):
    np.random.seed(seed)
    _w = jnp.asarray

    def _rec_inputs():
        import jax
        import jax.numpy as jnp
        _gk = jax.random.key(seed)
        x = -0.0005207 + 1.001 * jax.random.normal(jax.random.fold_in(_gk, 1), (8, 1024, 128), jnp.float32)
        _a = jax.random.bernoulli(jax.random.fold_in(_gk, 2), 0.015625, (1024, 1024))
        _a = jnp.logical_or(_a, jnp.swapaxes(_a, -1, -2))
        _a = jnp.logical_or(_a, jnp.eye(1024, dtype=bool))
        adj = _a.astype(jnp.int32)
        return (x, adj)
    x, adj = _rec_inputs()

    def _L0_gnn_setup():
        import jax, jax.numpy as jnp
        import numpy as np
        import math
        CHUNK = 128
        NUM_HEADS = 4
        EPS = 1e-05
        key = jax.random.key(seed)
        ks = jax.random.split(key, 12)
        B, N, F = (4, 1024, 128)
        x = jax.random.normal(ks[0], (B, N, F), dtype=jnp.float32)
        adj_matrix = jax.random.randint(ks[1], (N, N), 0, 2, dtype=jnp.int32)
        s = 1.0 / math.sqrt(F)
        Wq = jax.random.normal(ks[2], (F, F), dtype=jnp.float32) * s
        bq = jnp.zeros((F,), dtype=jnp.float32)
        Wk = jax.random.normal(ks[3], (F, F), dtype=jnp.float32) * s
        bk = jnp.zeros((F,), dtype=jnp.float32)
        Wv = jax.random.normal(ks[4], (F, F), dtype=jnp.float32) * s
        bv = jnp.zeros((F,), dtype=jnp.float32)
        Wo = jax.random.normal(ks[5], (F, F), dtype=jnp.float32) * s
        bo = jnp.zeros((F,), dtype=jnp.float32)
        gamma = jnp.ones((F,), dtype=jnp.float32)
        beta = jnp.zeros((F,), dtype=jnp.float32)
        return {'x': x, 'adj_matrix': adj_matrix, 'Wq': Wq, 'bq': bq, 'Wk': Wk, 'bk': bk, 'Wv': Wv, 'bv': bv, 'Wo': Wo, 'bo': bo, 'gamma': gamma, 'beta': beta}
    _L0_gnn_all = _L0_gnn_setup()
    _L0_gnn_in = {k: v for k, v in _L0_gnn_all.items() if k in ('Wq', 'bq', 'Wk', 'bk', 'Wv', 'bv', 'Wo', 'bo', 'gamma', 'beta')}
    del _L0_gnn_all

    def _L0_ffn_setup():
        import jax, jax.numpy as jnp
        import numpy as np
        B, S, D, E, H, K = (4, 2048, 128, 8, 256, 2)
        key = jax.random.key(seed)
        ks = jax.random.split(key, 6)
        x = jax.random.normal(ks[0], (B, S, D), jnp.float32)
        Wg = jax.random.normal(ks[1], (D, E), jnp.float32) * 0.02
        bg = jnp.zeros((E,), jnp.float32)
        W1 = jax.random.normal(ks[2], (E, D, H), jnp.float32) * 0.02
        b1 = jnp.zeros((E, H), jnp.float32)
        W2 = jax.random.normal(ks[3], (E, H, D), jnp.float32) * 0.02
        b2 = jnp.zeros((E, D), jnp.float32)
        return {'x': x, 'Wg': Wg, 'bg': bg, 'W1': W1, 'b1': b1, 'W2': W2, 'b2': b2}
    _L0_ffn_all = _L0_ffn_setup()
    _L0_ffn_in = {k: v for k, v in _L0_ffn_all.items() if k in ('Wg', 'bg', 'W1', 'b1', 'W2', 'b2')}
    del _L0_ffn_all
    return {'x': x, 'adj': adj, 'L0_gnn_Wq': _L0_gnn_in['Wq'], 'L0_gnn_bq': _L0_gnn_in['bq'], 'L0_gnn_Wk': _L0_gnn_in['Wk'], 'L0_gnn_bk': _L0_gnn_in['bk'], 'L0_gnn_Wv': _L0_gnn_in['Wv'], 'L0_gnn_bv': _L0_gnn_in['bv'], 'L0_gnn_Wo': _L0_gnn_in['Wo'], 'L0_gnn_bo': _L0_gnn_in['bo'], 'L0_gnn_gamma': _L0_gnn_in['gamma'], 'L0_gnn_beta': _L0_gnn_in['beta'], 'L0_ffn_Wg': _L0_ffn_in['Wg'], 'L0_ffn_bg': _L0_ffn_in['bg'], 'L0_ffn_W1': _L0_ffn_in['W1'], 'L0_ffn_b1': _L0_ffn_in['b1'], 'L0_ffn_W2': _L0_ffn_in['W2'], 'L0_ffn_b2': _L0_ffn_in['b2']}

def reference(x, adj, L0_gnn_Wq, L0_gnn_bq, L0_gnn_Wk, L0_gnn_bk, L0_gnn_Wv, L0_gnn_bv, L0_gnn_Wo, L0_gnn_bo, L0_gnn_gamma, L0_gnn_beta, L0_ffn_Wg, L0_ffn_bg, L0_ffn_W1, L0_ffn_b1, L0_ffn_W2, L0_ffn_b2):
    import jax
    import jax.numpy as jnp

    def _L0_gnn_ref(x, adj_matrix, Wq, bq, Wk, bk, Wv, bv, Wo, bo, gamma, beta):
        import jax, jax.numpy as jnp
        import numpy as np
        import math
        CHUNK = 128
        NUM_HEADS = 4
        EPS = 1e-05
        B, N, Fin = x.shape
        H = NUM_HEADS
        Dout = Wq.shape[0]
        Dh = Dout // H
        Nc = N // CHUNK
        q = (x @ Wq.T + bq).reshape(B, N, H, Dh).transpose(0, 2, 1, 3)
        k = (x @ Wk.T + bk).reshape(B, N, H, Dh).transpose(0, 2, 1, 3)
        v = (x @ Wv.T + bv).reshape(B, N, H, Dh).transpose(0, 2, 1, 3)
        kc = k.reshape(B, H, Nc, CHUNK, Dh)
        vc = v.reshape(B, H, Nc, CHUNK, Dh)
        scores = jnp.einsum('bhnd,bhjcd->bhnjc', q, kc) / jnp.sqrt(jnp.asarray(Dh, dtype=q.dtype))
        scores = jnp.clip(scores, -10.0, 10.0)
        mask = adj_matrix.reshape(N, Nc, CHUNK)[None, None]
        scores = jnp.where(mask == 0, jnp.asarray(-10.0, scores.dtype), scores)
        attn = jax.nn.softmax(scores, axis=-1)
        ctx = jnp.einsum('bhnjc,bhjcd->bhnd', attn, vc)
        ctx = ctx.transpose(0, 2, 1, 3).reshape(B, N, Dout)
        out = ctx @ Wo.T + bo
        out = out + x
        mu = jnp.mean(out, axis=-1, keepdims=True)
        var = jnp.mean(jnp.square(out - mu), axis=-1, keepdims=True)
        out = (out - mu) * jax.lax.rsqrt(var + EPS) * gamma + beta
        return out

    def _L0_ffn_ref(x, Wg, bg, W1, b1, W2, b2):
        import jax, jax.numpy as jnp
        import numpy as np
        B, S, D, E, H, K = (4, 2048, 128, 8, 256, 2)
        Bv, Sv, Dv = x.shape
        gate_scores = x @ Wg + bg
        _, idx = jax.lax.top_k(gate_scores, K)
        mask = jax.nn.one_hot(idx, E, dtype=x.dtype).sum(axis=-2)
        xf = x.reshape(-1, Dv)
        mf = mask.reshape(-1, E)
        h = jax.nn.gelu(jnp.einsum('td,edh->teh', xf, W1) + b1[None], approximate=False)
        y = jnp.einsum('teh,ehd->ted', h, W2) + b2[None]
        out = jnp.einsum('ted,te->td', y, mf)
        return out.reshape(Bv, Sv, Dv)
    x = x + _L0_gnn_ref(_layernorm(x, axis=-1), adj, L0_gnn_Wq, L0_gnn_bq, L0_gnn_Wk, L0_gnn_bk, L0_gnn_Wv, L0_gnn_bv, L0_gnn_Wo, L0_gnn_bo, L0_gnn_gamma, L0_gnn_beta)
    x = x + _L0_ffn_ref(_layernorm(x, axis=-1), L0_ffn_Wg, L0_ffn_bg, L0_ffn_W1, L0_ffn_b1, L0_ffn_W2, L0_ffn_b2)
    return x

_drawn_inputs = setup_inputs


def setup_inputs(seed=0):
    import zlib

    import numpy as np

    out = dict(_drawn_inputs(seed))
    spreads = {'L0_gnn_bq': (0.0, 0.1),
     'L0_gnn_bk': (0.0, 2.0),
     'L0_gnn_bv': (0.0, 0.1),
     'L0_gnn_bo': (0.0, 0.279),
     'L0_gnn_gamma': (1.0, 0.2),
     'L0_gnn_beta': (0.0, 0.1),
     'L0_ffn_bg': (0.0, 0.1),
     'L0_ffn_b1': (0.0, 0.574),
     'L0_ffn_b2': (0.0, 0.1)}
    factors = {}
    for name, (base, spread) in spreads.items():
        noise = np.random.default_rng([zlib.crc32(name.encode()), seed]).standard_normal(out[name].shape)
        drawn = base * np.exp(spread * noise) if base else spread * noise
        out[name] = jnp.asarray(drawn.astype(out[name].dtype))
    for name, factor in factors.items():
        out[name] = (out[name] * factor).astype(out[name].dtype)
    return out
```

```python
from contextlib import ExitStack

import numpy as np

import concourse.bass as bass
from concourse import mybir

F32 = mybir.dt.float32
F32R = mybir.dt.float32r
I32 = mybir.dt.int32
U32 = mybir.dt.uint32
ALU = mybir.AluOpType
ACT = mybir.ActivationFunctionType

P = 128
BATCH, SEQ, D = 8, 1024, 128
HEADS, DH = 4, 32
EXPERTS, HIDDEN = 8, 256
BLOCK = 512
TILES = BLOCK // P
BLOCKS = BATCH * SEQ // BLOCK
CHUNKS = SEQ // P
STEPS = CHUNKS * HEADS // 2
PAIRS = BLOCKS * STEPS
SLICES = EXPERTS * HIDDEN // P
BURST = SLICES // 2
HALF = TILES
VC = DH + 1
E_RING = 4
LN_EPS = 1e-5
SCORE_SCALE = 1.0 / float(np.sqrt(DH))
P_LOW = float(np.exp(np.float32(-10.0)))
P_HIGH = float(np.exp(np.float32(10.0)))

AV_LAG = 3
NORM_LAG = 4
FIRST, LAST = -3, BLOCKS + 2
LOOP_FROM, LOOP_TO = 5, 12

SHARED = [(0, "xnT", 2), (1, "gate", -2), (2, "q", 2), (3, "maskT", -2), (4, "k", 2), (5, "b2", -2),
          (6, "v", 2), (7, "ctxT", -1), (9, "proj", -1), (15, "x2T", -1)]


class Round:

    def __init__(self, i, c):
        self.i, self.c = i, c
        self.loop = not isinstance(i, int)
        self.u = None if self.loop else 2 * i + c

    def lin(self, per, add):
        return 2 * per * self.i + (per * self.c + add)

    def par(self, d=0):
        return (self.c + d) % 2

    def twos(self, d, per, add=0):
        return per * self.i + (per * ((self.c + d) // 2 + 1) + add)

    def has(self, d):
        return self.loop or 0 <= self.u + d < BLOCKS

    def pair(self, s, d=0):
        if not self.loop and not 0 <= STEPS * self.u + s + d < PAIRS:
            return None
        return self.lin(STEPS, s + d)

    def shared(self, name, back=0):
        def count(u, name):
            n = 0
            for r in range(FIRST, u + 1):
                for _, what, d in SHARED:
                    if 0 <= r + d < BLOCKS:
                        n += 1
                    if r == u and what == name:
                        return n
        if not self.loop:
            return count(self.u - back, name)
        per = len(SHARED)
        base = count(LOOP_FROM, name) - per * LOOP_FROM
        return self.lin(per, base - per * back)


def need(eng, sem, value):
    if isinstance(value, int) and value <= 0:
        return
    eng.wait_ge(sem, value)


def rounds(eng, body):
    for u in range(FIRST, LOOP_FROM):
        body(Round(u // 2, u % 2))
    with eng.Fori((LOOP_FROM - 1) // 2, LOOP_TO // 2) as i:
        body(Round(i, 1))
        body(Round(i, 2))
    for u in range(LOOP_TO + 1, LAST + 1):
        body(Round(u // 2, u % 2))


def graph_transformer_layer(nc, x, adjT, wqT, bq, wkT, bk, wvT, bv, woT, bo, gamma, beta,
                            wg, bg, w1, b1T, w2, b2, out):
    ctx = ExitStack()
    with ctx:
        def sb(name, shape, dt=F32):
            return ctx.enter_context(nc.sbuf_tensor(name, shape, dt))

        def sem(name):
            return ctx.enter_context(nc.semaphore(name))

        def sem2(name):
            return [sem(f"{name}_{k}") for k in range(2)]

        def by_block(ap):
            return ap.rearrange("(v t p) d -> v p t d", t=TILES, p=P)

        x_blocks = by_block(x.rearrange("b n d -> (b n) d"))
        out_blocks = by_block(out.rearrange("b n d -> (b n) d"))
        scratch = nc.dram_tensor("xn_plus_bo_scratch", (BLOCKS, P, TILES, D), F32).ap()

        ident = sb("ident", [P, P])
        top = sb("top", [P, CHUNKS, SEQ])
        top_i = top[:].bitcast(I32)
        w_hi = sb("w_hi", [P, 4, D], F32R)
        w_lo = sb("w_lo", [P, 4, D], F32R)
        wg_hi = sb("wg_hi", [P, EXPERTS], F32R)
        wg_lo = sb("wg_lo", [P, EXPERTS], F32R)
        w1_hi = sb("w1_hi", [P, SLICES * P], F32R)
        w1_lo = sb("w1_lo", [P, SLICES * P], F32R)
        w2_sb = sb("w2_sb", [P, SLICES, D])
        b2_sb = sb("b2_sb", [EXPERTS, D])
        b1_sb = sb("b1_sb", [P, SLICES])
        bq_sb = sb("bq_sb", [P, 1])
        bk_sb = sb("bk_sb", [P, 1])
        rows = sb("rows", [P, 4, D])
        bv_row, bo_row, gamma_row, beta_row = (rows[:, k:k + 1, :].to_broadcast([P, TILES, D]) for k in range(4))
        bg_row = sb("bg_row", [P, 1, EXPERTS])
        expert_no = sb("expert_no", [P, 1, EXPERTS])
        minus_half = sb("minus_half", [P, TILES])

        k_stack = sb("k_stack", [P, HEADS, SEQ], F32R)
        q_stack = [sb(f"q_stack{k}", [P, HEADS, BLOCK], F32R) for k in range(2)]
        v_aug = sb("v_aug", [P, CHUNKS, HEADS * VC])
        probs = sb("probs", [P, E_RING, 2, BLOCK])
        z_inv = sb("z_inv", [P, 4, TILES * 2])
        ctx_part = sb("ctx_part", [P, 2, TILES, 2, DH])
        ctx_sum = sb("ctx_sum", [P, 2, TILES, D])

        x_in = sb("x_in", [P, 2, TILES, D])
        xn = sb("xn", [P, TILES, D])
        xnbo = sb("xnbo", [P, TILES, D])
        xnT_hi = sb("xnT_hi", [P, BLOCK], F32R)
        xnT_lo = sb("xnT_lo", [P, BLOCK], F32R)
        q_hi = [sb(f"q_hi{k}", [P, BLOCK], F32R) for k in range(2)]
        q_lo = [sb(f"q_lo{k}", [P, BLOCK], F32R) for k in range(2)]
        k_hi = [sb(f"k_hi{k}", [P, BLOCK], F32R) for k in range(2)]
        k_lo = [sb(f"k_lo{k}", [P, BLOCK], F32R) for k in range(2)]
        v_new = [sb(f"v_new{k}", [P, HALF, HEADS * VC]) for k in range(2)]

        ctxT_hi = sb("ctxT_hi", [P, BLOCK], F32R)
        ctxT_lo = sb("ctxT_lo", [P, BLOCK], F32R)
        x_post = sb("x_post", [P, TILES, D])
        xnbo_post = sb("xnbo_post", [P, TILES, D])
        res = sb("res", [P, TILES, D])
        x2 = sb("x2", [P, TILES, D])
        xn2 = sb("xn2", [P, TILES, D])
        xn2T_hi = [sb(f"xn2T_hi{k}", [P, BLOCK], F32R) for k in range(2)]
        xn2T_lo = [sb(f"xn2T_lo{k}", [P, BLOCK], F32R) for k in range(2)]

        gates = sb("gates", [P, TILES, EXPERTS])
        best = sb("best", [P, TILES, 8])
        best_at = sb("best_at", [P, TILES, 8], U32)
        is_second = sb("is_second", [P, TILES, EXPERTS])
        chosen = sb("chosen", [P, 2, TILES, EXPERTS])
        chosenT = sb("chosenT", [EXPERTS, BLOCK])
        hidden = sb("hidden", [P, BURST, BLOCK])
        y_part = sb("y_part", [P, 2, TILES, D])
        y_sum = sb("y_sum", [P, 2, TILES, D])

        def bank(name):
            return ctx.enter_context(nc.psum_tensor(name, [P, BLOCK], F32))

        scores_ps = [bank(f"scores_ps{k}") for k in range(2)]
        ctx_ps = [bank(f"ctx_ps{k}") for k in range(2)]
        hidden_ps = [bank(f"hidden_ps{k}") for k in range(2)]
        y_ps = bank("y_ps")
        shared_ps = bank("shared_ps")

        consts_loaded = sem("consts_loaded")
        adj_loaded = sem("adj_loaded")
        ident_zeroed = sem("ident_zeroed")
        passed = sem("passed")
        pool_consts = sem("pool_consts")
        split_hi = sem("split_hi")
        weights_split = sem("weights_split")
        top_raw = sem("top_raw")
        top_ready = sem("top_ready")

        score_ready = sem("score_ready")
        exp_done = sem("exp_done")
        probs_ready = sem("probs_ready")
        ctx_ready = sem("ctx_ready")
        z_inverted = sem("z_inverted")
        ctx_scaled = sem("ctx_scaled")
        ctx_added = sem("ctx_added")

        shared_filled = sem("shared_filled")
        shared_drained = sem("shared_drained")
        hi_ready = {n: sem(f"hi_ready_{n}") for n in ("xnT", "q", "k", "ctxT", "x2T")}

        x_loaded = sem2("x_loaded")
        post_loaded = sem2("post_loaded")
        xnbo_stored = sem2("xnbo_stored")
        q_copied = sem2("q_copied")
        k_copied = sem2("k_copied")
        v_copied = sem2("v_copied")
        y_stored = sem2("y_stored")

        ln = {}
        for n in ("first", "second", "third"):
            ln[n] = dict(stats=sb(f"ln_stats_{n}", [P, TILES, 6]), mv=sb(f"ln_mv_{n}", [P, TILES, 2]),
                         rstd=sb(f"ln_rstd_{n}", [P, TILES]), s_stats=sem(f"ln_stats_ready_{n}"),
                         s_mv=sem(f"ln_mv_ready_{n}"), s_eps=sem(f"ln_eps_added_{n}"),
                         s_rstd=sem(f"ln_rstd_ready_{n}"), s_out=sem(f"ln_out_ready_{n}"))

        xnbo_ready = sem("xnbo_ready")
        x_beta_ready = sem("x_beta_ready")
        res_ready = sem("res_ready")
        res_scaled = sem("res_scaled")
        x2_ready = sem("x2_ready")

        gates_ready = sem("gates_ready")
        best_ready = sem("best_ready")
        best_at_ready = sem("best_at_ready")
        ranks_ready = sem("ranks_ready")
        chosen_ready = sem("chosen_ready")

        hidden_pre = sem("hidden_pre")
        hidden_ready = sem("hidden_ready")
        hidden_used = sem("hidden_used")
        y_masked = sem("y_masked")
        y_added = sem("y_added")

        def need_apart(eng, sem_, value):
            need(eng, sem_, value)
            eng.sem_inc(passed, 1)

        W_Q, W_K, W_V, W_O = range(4)
        KEYS = HALF * P

        block = ctx.enter_context(nc.Block())

        @block.sync
        def _(sp):
            def load(dst, src):
                sp.dma_start(dst, src).then_inc(consts_loaded, 16)

            def row(ap, n):
                return ap.rearrange("(a n) -> a n", a=1).to_broadcast([P, n])

            stage = probs[:].rearrange("p a b c -> p (a b c)")
            for k, w in enumerate((wqT, wkT, wvT, woT)):
                load(stage[:, 2048 + k * D:2048 + (k + 1) * D], w)
            for k, b in enumerate((bv, bo, gamma, beta)):
                load(rows[:, k, :], row(b, D))
            load(bg_row[:, 0, :], row(bg, EXPERTS))
            load(bq_sb[:], bq.rearrange("(p a) -> p a", a=1))
            load(bk_sb[:], bk.rearrange("(p a) -> p a", a=1))
            load(stage[:, 2560:2560 + EXPERTS], wg)
            load(stage[:, 0:2048].rearrange("p (e h) -> p e h", e=EXPERTS), w1.rearrange("e d h -> d e h"))
            load(b1_sb[:], b1T)
            load(b2_sb[:], b2)
            load(w2_sb[:].rearrange("p (e k) d -> p e k d", e=EXPERTS), w2.rearrange("e (k p) d -> p e k d", p=P))
            for c in range(CHUNKS):
                sp.dma_start(top_i[:, c, :], adjT[c * P:(c + 1) * P, :]).then_inc(adj_loaded, 16)

            def body(u):
                copy_q = u.has(1)
                if copy_q:
                    v = u.par(1)
                    need_apart(sp, shared_drained, u.shared("q", back=1))
                    need(sp, score_ready, u.lin(2 * STEPS, 0) if u.has(-1) else 0)
                    for h in range(HEADS):
                        rows_of = slice(DH * h, DH * (h + 1))
                        for g, part in enumerate((q_hi, q_hi, q_lo, q_lo)):
                            sp.dma_start(q_stack[v][DH * g:DH * (g + 1), h, :].bitcast(F32),
                                         part[v][rows_of, :].bitcast(F32)).then_inc(q_copied[v], 16)

                def copy_kv():
                    v = u.par(1)
                    step = 0 if v else HALF * 2
                    need_apart(sp, shared_drained, u.shared("v", back=1))
                    need(sp, score_ready, u.lin(2 * STEPS, 2 * step) if u.has(-1) else 0)
                    for h in range(HEADS):
                        rows_of = slice(DH * h, DH * (h + 1))
                        for g, part in enumerate((k_hi, k_lo, k_hi, k_lo)):
                            sp.dma_start(k_stack[DH * g:DH * (g + 1), h, KEYS * v:KEYS * (v + 1)].bitcast(F32),
                                         part[v][rows_of, :].bitcast(F32)).then_inc(k_copied[v], 16)
                    need(sp, ctx_ready, u.lin(STEPS, step) if u.has(-1) else 0)
                    sp.dma_start(v_aug[:, HALF * v:HALF * (v + 1), :], v_new[v][:]).then_inc(v_copied[v], 16)

                if u.has(1) and u.par(1):
                    copy_kv()
                if u.has(3):
                    need(sp, ln["first"]["s_out"], u.lin(1, 2))
                    sp.dma_start(x_in[:, u.par(3), :, :], x_blocks[u.lin(1, 3)]).then_inc(x_loaded[u.par(3)], 16)
                if u.has(-1):
                    need(sp, x2_ready, u.lin(1, -1))
                    need(sp, xnbo_stored[u.par(-1)], u.twos(-1, 16))
                    sp.dma_start(x_post[:], x_blocks[u.lin(1, -1)]).then_inc(post_loaded[u.par(-1)], 16)
                    sp.dma_start(xnbo_post[:], scratch[u.lin(1, -1)]).then_inc(post_loaded[u.par(-1)], 16)
                if u.has(1) and not u.par(1):
                    copy_kv()
                if u.has(-3):
                    need(sp, y_added, u.lin(EXPERTS, -2 * EXPERTS))
                    sp.dma_start(out_blocks[u.lin(1, -3)], y_sum[:, u.par(-3), :, :]).then_inc(y_stored[u.par(-3)], 16)
                if u.has(3):
                    need(sp, xnbo_ready, u.lin(1, 4))
                    sp.dma_start(scratch[u.lin(1, 3)], xnbo[:]).then_inc(xnbo_stored[u.par(3)], 16)

            rounds(sp, body)
            for k in range(2):
                sp.wait_ge(y_stored[k], 16 * BLOCKS // 2)
                sp.wait_ge(xnbo_stored[k], 16 * BLOCKS // 2)

        @block.tensor
        def _(pe):
            def fill(name, u, emit):
                if name is None:
                    return
                need(pe, shared_drained, u.shared(name) - 1 if not u.loop else u.shared(name) + (-1))
                emit().then_inc(shared_filled, 1)

            def transposes(src):
                for t in range(TILES):
                    last = pe.transpose(shared_ps[:, t * P:(t + 1) * P], src[:, t, :], ident[:])
                return last

            def three(dst, l_hi, l_lo, r_hi, r_lo):
                pe.matmul(dst, l_hi, r_hi, start=True, stop=False)
                pe.matmul(dst, l_hi, r_lo, start=False, stop=False)
                return pe.matmul(dst, l_lo, r_hi, start=False, stop=True)

            def shared_use(name, u):
                if name == "xnT":
                    need(pe, ln["first"]["s_out"], u.lin(1, 3))
                    fill(name, u, lambda: transposes(xn))
                elif name in ("q", "k"):
                    w = W_Q if name == "q" else W_K
                    if name == "q":
                        need(pe, weights_split, 1)
                    fill(name, u, lambda: three(shared_ps[:], w_hi[:, w, :], w_lo[:, w, :], xnT_hi[:], xnT_lo[:]))
                elif name == "v":
                    def emit():
                        for t in range(TILES):
                            cols = slice(t * P, (t + 1) * P)
                            last = three(shared_ps[:, cols], xnT_hi[:, cols], xnT_lo[:, cols],
                                         w_hi[:, W_V, :], w_lo[:, W_V, :])
                        return last
                    fill(name, u, emit)
                elif name == "ctxT":
                    need(pe, ctx_added, u.lin(STEPS - 2, 0))
                    fill(name, u, lambda: transposes(ctx_sum[:, u.par(-1), :, :]))
                elif name == "proj":
                    def emit():
                        for t in range(TILES):
                            cols = slice(t * P, (t + 1) * P)
                            last = three(shared_ps[:, cols], ctxT_hi[:, cols], ctxT_lo[:, cols],
                                         w_hi[:, W_O, :], w_lo[:, W_O, :])
                        return last
                    fill(name, u, emit)
                elif name == "x2T":
                    need(pe, ln["third"]["s_out"], u.lin(1, 0))
                    fill(name, u, lambda: transposes(xn2))
                elif name == "gate":
                    def emit():
                        b = u.par(-2)
                        for t in range(TILES):
                            cols = slice(t * P, (t + 1) * P)
                            dst = shared_ps[:, t * EXPERTS:(t + 1) * EXPERTS]
                            pe.matmul(dst, xn2T_hi[b][:, cols], wg_hi[:], start=True, stop=False)
                            pe.matmul(dst, xn2T_hi[b][:, cols], wg_lo[:], start=False, stop=False)
                            pe.matmul(dst, xn2T_lo[b][:, cols], wg_hi[:], start=False, stop=False)
                            last = pe.matmul(dst, xn2T_lo[b][:, cols], wg_lo[:], start=False, stop=True)
                        return last
                    fill(name, u, emit)
                elif name == "maskT":
                    need(pe, chosen_ready, u.lin(1, -1))

                    def emit():
                        for t in range(TILES):
                            last = pe.transpose(shared_ps[0:EXPERTS, t * P:(t + 1) * P],
                                                chosen[:, u.par(-2), t, :], ident[:])
                        return last
                    fill(name, u, emit)
                elif name == "b2":
                    def emit():
                        for t in range(TILES):
                            last = pe.matmul(shared_ps[:, t * P:(t + 1) * P], chosenT[:, t * P:(t + 1) * P],
                                             b2_sb[:], start=True, stop=True)
                        return last
                    fill(name, u, emit)

            def scores(u, s, t, hh):
                h, j = 2 * (s % 2) + hh, s // 2
                if hh == 0 and s == 0:
                    pe.wait_ge(q_copied[u.par()], u.twos(0, 256))
                    if u.par() == 0:
                        pe.wait_ge(k_copied[0], u.twos(0, 256))
                if hh == 0 and s == 2 * HALF and u.par() == 0:
                    pe.wait_ge(k_copied[1], u.twos(1, 256))
                need(pe, exp_done, u.lin(2 * STEPS, 2 * s - 1 + hh))
                pe.matmul(scores_ps[hh][:], k_stack[:, h, j * P:(j + 1) * P], q_stack[u.par()][:, h, :],
                          start=True, stop=True).then_inc(score_ready, 1)

            def weighted_sum(u, s, part):
                back = s - AV_LAG
                ps, rnd = back % STEPS, 0 if back >= 0 else -1
                j, hp = ps // 2, ps % 2
                if part == 0:
                    if ps == 0:
                        pe.wait_ge(v_copied[0], u.twos(rnd, 16)) if u.par(rnd) == 0 else None
                    if ps == 2 * HALF and u.par(rnd) == 0:
                        pe.wait_ge(v_copied[1], u.twos(rnd + 1, 16))
                    need(pe, probs_ready, u.lin(STEPS, back + 1))
                    need(pe, ctx_scaled, u.lin(STEPS, back - 1))
                bank_ = ctx_ps[ps % 2]
                for t in range(2 * part, 2 * part + 2):
                    for hh in range(2):
                        at = (2 * t + hh) * VC
                        h = 2 * hp + hh
                        last = pe.matmul(bank_[:, at:at + VC], probs[:, ps % E_RING, hh, t * P:(t + 1) * P],
                                         v_aug[:, j, h * VC:(h + 1) * VC], start=True, stop=True)
                if part == 1:
                    last.then_inc(ctx_ready, 1)

            def first_products(u, k0):
                b = u.par(-2)
                if k0 == 0:
                    need(pe, shared_drained, u.shared("x2T", back=1))
                for k in range(k0, k0 + BURST):
                    need(pe, hidden_ready, u.lin(SLICES, k - 2 * SLICES - 1))
                    cols = slice(k * P, (k + 1) * P)
                    three(hidden_ps[k % 2][:], w1_hi[:, cols], w1_lo[:, cols], xn2T_hi[b][:], xn2T_lo[b][:])\
                        .then_inc(hidden_pre, 1)

            def second_product(u, k, back):
                need(pe, hidden_ready, u.lin(SLICES, k + 1 - back * SLICES))
                if k % 2 == 0:
                    need(pe, y_masked, u.lin(EXPERTS, k // 2 - back * EXPERTS))
                for t in range(TILES):
                    last = pe.matmul(y_ps[:, t * P:(t + 1) * P], hidden[:, k % BURST, t * P:(t + 1) * P],
                                     w2_sb[:, k, :], start=(k % 2 == 0 and t == 0),
                                     stop=(k % 2 == 1 and t == TILES - 1), skip_group_check=True)
                last.then_inc(hidden_used, 1)

            pe.wait_ge(pool_consts, 1)

            def body(u):
                for s in range(STEPS):
                    now, before = u.pair(s), u.pair(s, -AV_LAG)
                    if now is not None:
                        scores(u, s, now, 0)
                    if before is not None:
                        weighted_sum(u, s, 0)
                    if now is not None:
                        scores(u, s, now, 1)
                    if before is not None:
                        weighted_sum(u, s, 1)
                    if s < BURST and u.has(-3):
                        second_product(u, BURST + s, 3)
                    if s >= BURST and u.has(-2):
                        second_product(u, s - BURST, 2)
                    for at, name, d in SHARED:
                        if at == s and u.has(d):
                            shared_use(name, u)
                    if s in (BURST - 1, STEPS - 1) and u.has(-2):
                        first_products(u, 0 if s < BURST else BURST)

            rounds(pe, body)

        @block.scalar
        def _(act):
            act.wait_ge(consts_loaded, 16 * 16)

            def hi_part(u, name, dst, free, bias=None):
                d = dict((n, d) for _, n, d in SHARED)[name]
                need(act, shared_filled, u.shared(name))
                for s_, v_ in free:
                    need(act, s_, v_)
                if bias is None:
                    ins = nc.scalar.activation(dst, shared_ps[:], ACT.Copy)
                else:
                    ins = nc.scalar.activation(dst, shared_ps[:], ACT.Identity, bias=bias)
                ins.then_inc(hi_ready[name], 1)

            def gelu(u, k0):
                for k in range(k0, k0 + BURST):
                    need(act, hidden_pre, u.lin(SLICES, k + 1 - 2 * SLICES))
                    need(act, hidden_used, u.lin(SLICES, k + 1 - BURST - 2 * SLICES))
                    nc.scalar.activation(hidden[:, k % BURST, :], hidden_ps[k % 2][:], ACT.Gelu,
                                         bias=b1_sb[:, k:k + 1]).then_inc(hidden_ready, 1)

            def body(u):
                for s in range(STEPS):
                    if u.pair(s) is not None:
                        for hh in range(2):
                            need(act, score_ready, u.lin(2 * STEPS, 2 * s + hh + 1))
                            if hh == 0:
                                need(act, ctx_ready, u.lin(STEPS, s + 1 - E_RING))
                            nc.scalar.activation(probs[:, s % E_RING, hh, :], scores_ps[hh][:], ACT.Exp,
                                                 scale=SCORE_SCALE).then_inc(exp_done, 1)
                    for at, name, d in SHARED:
                        if at != s or not u.has(d):
                            continue
                        b = u.par(d)
                        if name == "xnT":
                            hi_part(u, name, xnT_hi[:], [(shared_filled, u.shared("v", back=1) if u.has(1) else 0)])
                        elif name == "q":
                            hi_part(u, name, q_hi[b][:], [(q_copied[b], u.twos(d - 2, 256))], bq_sb[:, 0:1])
                        elif name == "k":
                            hi_part(u, name, k_hi[b][:], [(k_copied[b], u.twos(d - 2, 256))], bk_sb[:, 0:1])
                        elif name == "ctxT":
                            hi_part(u, name, ctxT_hi[:], [(shared_filled, u.shared("proj", back=1) if u.has(-2) else 0)])
                        elif name == "x2T":
                            hi_part(u, name, xn2T_hi[b][:], [(hidden_pre, u.lin(SLICES, -2 * SLICES))])
                    if s in (BURST - 1, STEPS - 1) and u.has(-2):
                        gelu(u, 0 if s < BURST else BURST)

            rounds(act, body)

        @block.vector
        def _(dve):
            def filled(u, name):
                need(dve, shared_filled, u.shared(name))

            def lo_part(u, name, dst, hi, bias=None):
                d = dict((n, d) for _, n, d in SHARED)[name]
                need(dve, hi_ready[name], u.lin(1, d + 1))
                if bias is None:
                    ins = dve.tensor_tensor(dst, shared_ps[:], hi.bitcast(F32), ALU.subtract)
                else:
                    ins = dve.scalar_tensor_tensor(out=dst, in0=shared_ps[:], scalar=bias, in1=hi.bitcast(F32),
                                                   op0=ALU.add, op1=ALU.subtract)
                ins.then_inc(shared_drained, 1)

            def statistics(l, src, count):
                for t in range(TILES):
                    last = dve.bn_stats(l["stats"][:, t, :], src[:, t, :])
                last.then_inc(l["s_stats"], 1)
                need_apart(dve, l["s_stats"], count)
                for t in range(TILES):
                    last = dve.bn_aggr(l["mv"][:, t, :], l["stats"][:, t, :])
                last.then_inc(l["s_mv"], 1)

            def normalise(l, dst, src, count):
                dve.wait_ge(l["s_rstd"], count)
                for t in range(TILES):
                    last = dve.tensor_scalar(dst[:, t, :], src[:, t, :], l["mv"][:, t, 0:1], l["rstd"][:, t:t + 1],
                                             ALU.subtract, ALU.mult)
                last.then_inc(l["s_out"], 1)

            stage = probs[:].rearrange("p a b c -> p (a b c)")
            dve.wait_ge(consts_loaded, 16 * 16)
            parts = [(w_hi[:].rearrange("p a b -> p (a b)"), w_lo[:].rearrange("p a b -> p (a b)"), stage[:, 2048:2560]),
                     (wg_hi[:], wg_lo[:], stage[:, 2560:2560 + EXPERTS]),
                     (w1_hi[:], w1_lo[:], stage[:, 0:2048])]
            for hi, lo, src in parts:
                dve.tensor_copy(hi, src).then_inc(split_hi, 1)
            for n, (hi, lo, src) in enumerate(parts):
                dve.wait_ge(split_hi, n + 1)
                dve.tensor_tensor(lo, src, hi.bitcast(F32), ALU.subtract).then_inc(weights_split, 1)
            for k in range(2):
                dve.memset(v_new[k][:].rearrange("p j (h c) -> p j h c", c=VC)[:, :, :, DH:VC], 1.0)

            def mask_chunk(j):
                dve.wait_ge(adj_loaded, 16 * CHUNKS)
                dve.tensor_scalar(top[:, j, :], top_i[:, j, :], 0.0, P_HIGH, ALU.not_equal, ALU.mult).then_inc(top_raw, 1)
                dve.wait_ge(top_raw, j + 1)
                dve.tensor_scalar(top[:, j, :], top[:, j, :], P_LOW, None, ALU.max).then_inc(top_ready, 1)

            def probabilities(u, s):
                back = s - 1
                ps, nb = back % STEPS, u.par(0 if back >= 0 else -1)
                j = ps // 2
                if not u.loop and u.u <= 1:
                    dve.wait_ge(top_ready, j + 1)
                need(dve, exp_done, u.lin(2 * STEPS, 2 * back + 2))
                e = probs[:, ps % E_RING, :, :]
                bound = top[:, j:j + 1, nb * BLOCK:(nb + 1) * BLOCK].to_broadcast([P, 2, BLOCK])
                dve.scalar_tensor_tensor(out=e, in0=e, scalar=P_LOW, in1=bound, op0=ALU.max, op1=ALU.min)\
                    .then_inc(probs_ready, 1)

            def by_head(ap):
                return ap.rearrange("p (t h c) -> p t h c", t=TILES, h=2)

            def invert_sums(u, s):
                back = s - NORM_LAG
                ps = back % STEPS
                need(dve, ctx_ready, u.lin(STEPS, back + 1))
                src = by_head(ctx_ps[ps % 2][:, 0:TILES * 2 * VC])[:, :, :, DH]
                dve.reciprocal(z_inv[:, ps % 4, :].rearrange("p (t h) -> p t h", h=2), src).then_inc(z_inverted, 1)

            def scale_context(u, s):
                back = s - NORM_LAG
                ps, rnd = back % STEPS, 0 if back >= 0 else -1
                hp = ps % 2
                src = by_head(ctx_ps[ps % 2][:, 0:TILES * 2 * VC])[:, :, :, 0:DH]
                inv = z_inv[:, ps % 4, :].rearrange("p (t h c) -> p t h c", h=2, c=1).to_broadcast([P, TILES, 2, DH])
                if ps < 2:
                    if u.loop or u.u + rnd >= 2:
                        need(dve, hi_ready["ctxT"], u.lin(1, rnd - 1))
                    dst = ctx_sum[:, u.par(rnd), :, hp * 2 * DH:(hp + 1) * 2 * DH].rearrange("p t (h c) -> p t h c", h=2)
                else:
                    if ps >= 4:
                        need(dve, ctx_added, u.lin(STEPS - 2, (STEPS - 2) * rnd + ps - 3))
                    else:
                        need(dve, ctx_added, u.lin(STEPS - 2, (STEPS - 2) * rnd))
                    dst = ctx_part[:, ps % 2, :, :, :]
                need(dve, z_inverted, u.lin(STEPS, back + 1))
                dve.tensor_tensor(dst, src, inv, ALU.mult).then_inc(ctx_scaled, 1)

            def mask_expert(u, e, back):
                need(dve, hidden_used, u.lin(SLICES, 2 * e + 2 - back * SLICES))
                need(dve, y_added, u.lin(EXPERTS, e - 1 - back * EXPERTS))
                m = chosen[:, u.par(-back), :, e:e + 1].to_broadcast([P, TILES, D])
                y = y_ps[:].rearrange("p (t d) -> p t d", t=TILES)
                dve.tensor_tensor(y_part[:, e % 2, :, :], y, m, ALU.mult).then_inc(y_masked, 1)

            def drain(u, name):
                ps3 = shared_ps[:].rearrange("p (t d) -> p t d", t=TILES)
                if name == "xnT":
                    lo_part(u, name, xnT_lo[:], xnT_hi[:])
                elif name == "q":
                    b = u.par(2)
                    lo_part(u, name, q_lo[b][:], q_hi[b][:], bq_sb[:, 0:1])
                elif name == "k":
                    b = u.par(2)
                    lo_part(u, name, k_lo[b][:], k_hi[b][:], bk_sb[:, 0:1])
                elif name == "v":
                    b = u.par(2)
                    filled(u, name)
                    need(dve, v_copied[b], u.twos(0, 16))
                    dve.tensor_tensor(v_new[b][:].rearrange("p j (h c) -> p j h c", c=VC)[:, :, :, 0:DH],
                                      ps3.rearrange("p t (h c) -> p t h c", c=DH),
                                      bv_row.rearrange("p t (h c) -> p t h c", c=DH), ALU.add)\
                        .then_inc(shared_drained, 1)
                elif name == "ctxT":
                    lo_part(u, name, ctxT_lo[:], ctxT_hi[:])
                elif name == "proj":
                    filled(u, name)
                    need(dve, post_loaded[u.par(-1)], u.twos(-1, 32))
                    need(dve, x2_ready, u.lin(1, -1))
                    dve.tensor_tensor(res[:], ps3, xnbo_post[:], ALU.add).then_inc(shared_drained, 1)
                    dve.wait_ge(shared_drained, u.shared(name))
                    statistics(ln["second"], res, u.lin(1, 0))
                elif name == "x2T":
                    b = u.par(-1)
                    lo_part(u, name, xn2T_lo[b][:], xn2T_hi[b][:])
                elif name == "gate":
                    filled(u, name)
                    n = u.lin(1, -1)
                    g = shared_ps[:, 0:TILES * EXPERTS].rearrange("p (t e) -> p t e", e=EXPERTS)
                    dve.tensor_tensor(gates[:], g, bg_row[:].to_broadcast([P, TILES, EXPERTS]), ALU.add)\
                        .then_inc(shared_drained, 1)
                    need_apart(dve, shared_drained, u.shared(name))
                    for t in range(TILES):
                        last = dve.max(best[:, t, :], gates[:, t, :])
                    last.then_inc(best_ready, 1)
                    need_apart(dve, best_ready, n)
                    for t in range(TILES):
                        last = dve.max_index(best_at[:, t, :], best[:, t, :], gates[:, t, :])
                    last.then_inc(best_at_ready, 1)
                    dve.wait_ge(best_at_ready, n)
                    no = expert_no[:].to_broadcast([P, TILES, EXPERTS])
                    one, two = (best_at[:, :, k:k + 1].to_broadcast([P, TILES, EXPERTS]) for k in range(2))
                    c = chosen[:, u.par(-2), :, :]
                    dve.tensor_tensor(c, no, one, ALU.is_equal)
                    dve.tensor_tensor(is_second[:], no, two, ALU.is_equal).then_inc(ranks_ready, 1)
                    dve.wait_ge(ranks_ready, n)
                    dve.tensor_tensor(c, c, is_second[:], ALU.add).then_inc(chosen_ready, 1)
                elif name == "maskT":
                    filled(u, name)
                    dve.tensor_copy(chosenT[:], shared_ps[0:EXPERTS, :]).then_inc(shared_drained, 1)
                elif name == "b2":
                    filled(u, name)
                    need(dve, y_stored[u.par(-2)], u.twos(-4, 16))
                    dve.tensor_tensor(y_sum[:, u.par(-2), :, :], ps3, x2[:], ALU.add).then_inc(shared_drained, 1)

            dve.wait_ge(pool_consts, 2)

            def body(u):
                for s in range(STEPS):
                    if not u.loop and u.u == 0 and s % 2 == 0:
                        mask_chunk(s // 2)
                    old = u.pair(s, -NORM_LAG)
                    if old is not None:
                        invert_sums(u, s)
                    if u.pair(s, -1) is not None:
                        probabilities(u, s)
                    if old is not None:
                        scale_context(u, s)
                    if s % 2 == 0 and s <= 8 and u.has(-3):
                        mask_expert(u, 3 + s // 2, 3)
                    if s % 2 == 0 and s >= 10 and u.has(-2):
                        mask_expert(u, (s - 10) // 2, 2)
                    for at, name, d in SHARED:
                        if at == s - 1 and u.has(d):
                            drain(u, name)
                        if at == STEPS - 1 and s == 0 and u.has(d - 1):
                            drain(previous(u), name)
                    if s == 11 and u.has(-1):
                        normalise(ln["second"], res, res, u.lin(1, 0))
                    if s == 12 and u.has(3):
                        need(dve, x_loaded[u.par(3)], u.twos(3, 16))
                        statistics(ln["first"], x_in[:, u.par(3), :, :], u.lin(1, 4))
                    if s == 13 and u.has(-1):
                        need(dve, x2_ready, u.lin(1, 0))
                        statistics(ln["third"], x2, u.lin(1, 0))
                    if s == 14 and u.has(-1):
                        need(dve, shared_filled, u.shared("x2T", back=1) if u.has(-2) else 0)
                        normalise(ln["third"], xn2, x2, u.lin(1, 0))
                    if s == 15 and u.has(3):
                        need(dve, shared_filled, u.shared("xnT") if u.has(2) else 0)
                        need(dve, xnbo_ready, u.lin(1, 3))
                        normalise(ln["first"], xn, x_in[:, u.par(3), :, :], u.lin(1, 4))

            def previous(u):
                return Round(u.i, u.c - 1)

            rounds(dve, body)

        @block.gpsimd
        def _(pool):
            nc.gpsimd.memset(ident[:], 0.0).then_inc(ident_zeroed, 1)
            nc.gpsimd.memset(minus_half[:], -0.5)
            pool.wait_ge(ident_zeroed, 1)
            nc.gpsimd.affine_select(out=ident[:], in_=ident[:], compare_op=ALU.not_equal, fill=1.0, base=0,
                                    pattern=[[-1, P]], channel_multiplier=1).then_inc(pool_consts, 1)
            for e in range(EXPERTS):
                last = nc.gpsimd.memset(expert_no[:, :, e:e + 1], float(e))
            last.then_inc(pool_consts, 1)
            pool.wait_ge(consts_loaded, 16 * 16)
            pool.wait_ge(pool_consts, 2)

            def root(l, count):
                need_apart(pool, l["s_mv"], count)
                nc.gpsimd.tensor_scalar(l["rstd"][:], l["mv"][:, :, 1], LN_EPS, None, ALU.add).then_inc(l["s_eps"], 1)
                pool.wait_ge(l["s_eps"], count)
                nc.gpsimd.tensor_tensor(l["rstd"][:], l["rstd"][:], minus_half[:], ALU.pow).then_inc(l["s_rstd"], 1)

            def add_context(u, s):
                back = s - NORM_LAG
                ps, rnd = back % STEPS, 0 if back >= 0 else -1
                if ps < 2:
                    return
                hp = ps % 2
                need(pool, ctx_scaled, u.lin(STEPS, back + 1))
                need(pool, ctx_added, u.lin(STEPS - 2, (STEPS - 2) * rnd + ps - 3))
                dst = ctx_sum[:, u.par(rnd), :, hp * 2 * DH:(hp + 1) * 2 * DH]
                nc.gpsimd.tensor_tensor(dst, dst, ctx_part[:, ps % 2, :, :, :].rearrange("p t h c -> p t (h c)"),
                                        ALU.add).then_inc(ctx_added, 1)

            def add_expert(u, e, back):
                need(pool, y_masked, u.lin(EXPERTS, e + 1 - back * EXPERTS))
                need(pool, y_added, u.lin(EXPERTS, e - back * EXPERTS))
                dst = y_sum[:, u.par(-back), :, :]
                nc.gpsimd.tensor_tensor(dst, dst, y_part[:, e % 2, :, :], ALU.add).then_inc(y_added, 1)

            def body(u):
                for s in range(STEPS):
                    if u.pair(s, -NORM_LAG) is not None:
                        add_context(u, s)
                    if s % 2 == 0 and s <= 8 and u.has(-3):
                        add_expert(u, 3 + s // 2, 3)
                    if s % 2 == 0 and s >= 10 and u.has(-2):
                        add_expert(u, (s - 10) // 2, 2)
                    if s == 5 and u.has(-1):
                        need(pool, post_loaded[u.par(-1)], u.twos(-1, 32))
                        nc.gpsimd.tensor_tensor(x_post[:], x_post[:], beta_row, ALU.add).then_inc(x_beta_ready, 1)
                    if s == 10 and u.has(-1):
                        root(ln["second"], u.lin(1, 0))
                    if s == 11 and u.has(-1):
                        need(pool, ln["second"]["s_out"], u.lin(1, 0))
                        nc.gpsimd.tensor_tensor(res[:], res[:], gamma_row, ALU.mult).then_inc(res_scaled, 1)
                        need(pool, res_scaled, u.lin(1, 0))
                        need(pool, x_beta_ready, u.lin(1, 0))
                        if u.has(-2):
                            need(pool, shared_drained, u.shared("b2"))
                        nc.gpsimd.tensor_tensor(x2[:], res[:], x_post[:], ALU.add).then_inc(x2_ready, 1)
                    if s == 12 and u.has(3):
                        root(ln["first"], u.lin(1, 4))
                    if s == 13 and u.has(-1):
                        root(ln["third"], u.lin(1, 0))
                    if s == 15 and u.has(3):
                        need(pool, ln["first"]["s_out"], u.lin(1, 4))
                        need(pool, xnbo_stored[u.par(2)], u.twos(2, 16))
                        nc.gpsimd.tensor_tensor(xnbo[:], xn[:], bo_row, ALU.add).then_inc(xnbo_ready, 1)

            rounds(pool, body)


def kernel(x, adj, L0_gnn_Wq, L0_gnn_bq, L0_gnn_Wk, L0_gnn_bk, L0_gnn_Wv, L0_gnn_bv, L0_gnn_Wo, L0_gnn_bo,
           L0_gnn_gamma, L0_gnn_beta, L0_ffn_Wg, L0_ffn_bg, L0_ffn_W1, L0_ffn_b1, L0_ffn_W2, L0_ffn_b2):
    import concourse.bacc as bacc
    from concourse.bass_utils import run_bass_kernel_spmd

    laid = dict(x=x, adjT=np.asarray(adj).T, wqT=np.asarray(L0_gnn_Wq).T, bq=L0_gnn_bq,
                wkT=np.asarray(L0_gnn_Wk).T, bk=L0_gnn_bk, wvT=np.asarray(L0_gnn_Wv).T, bv=L0_gnn_bv,
                woT=np.asarray(L0_gnn_Wo).T, bo=L0_gnn_bo, gamma=L0_gnn_gamma, beta=L0_gnn_beta,
                wg=L0_ffn_Wg, bg=L0_ffn_bg, w1=L0_ffn_W1,
                b1T=np.asarray(L0_ffn_b1).reshape(SLICES, P).T, w2=L0_ffn_W2, b2=L0_ffn_b2)
    nc = bacc.Bacc("TRN2", target_bir_lowering=False, num_devices=1)
    arrays, args = {}, []
    for name, value in laid.items():
        a = np.ascontiguousarray(value)
        arrays[f"in_{name}"] = a
        args.append(nc.dram_tensor(f"in_{name}", a.shape, mybir.dt.from_np(a.dtype), kind="ExternalInput").ap())
    out = nc.dram_tensor("out", (BATCH, SEQ, D), F32, kind="ExternalOutput").ap()
    graph_transformer_layer(nc, *args, out)
    results = run_bass_kernel_spmd(nc, [arrays], core_ids=[0])
    return results.results[0]["out"]
```

```python
from contextlib import ExitStack

import numpy as np

import concourse.bass as bass
from concourse import mybir

F32 = mybir.dt.float32
F32R = mybir.dt.float32r
I32 = mybir.dt.int32
U32 = mybir.dt.uint32
ALU = mybir.AluOpType
ACT = mybir.ActivationFunctionType

P = 128
BATCH, SEQ, D = 8, 1024, 128
HEADS, DH = 4, 32
EXPERTS, HIDDEN = 8, 256
BLOCK = 512
TILES = BLOCK // P
BLOCKS = BATCH * SEQ // BLOCK
CHUNKS = SEQ // P
STEPS = CHUNKS * HEADS // 2
SQUARES = BLOCK // DH
SLICES = EXPERTS * HIDDEN // P
BURST = SLICES // 2
HALF = TILES
E_RING = 4
LN_EPS = 1e-5
SCORE_SCALE = 1.0 / float(np.sqrt(DH))
P_LOW = float(np.exp(np.float32(-10.0)))
P_HIGH = float(np.exp(np.float32(10.0)))

CONTEXT_LAG, TURN_LAG, SCALE_LAG = 3, 4, 5
BURST_BANK = (0, 1, 0, 1, 2, 0, 1, 2)
BURST_BEFORE = (None, None, 0, 1, None, 2, 3, 4)
Y_BANK = (0, 1, 0, 2) * 2
FIRST, LAST = -3, BLOCKS + 2
LOOP_FROM, LOOP_TO = 5, 12

SHARED = [(0, "xnT", 2), (1, "gate", -2), (2, "k", 2), (3, "maskT", -2), (4, "v", 2), (5, "b2", -2),
          (6, "q", 2), (9, "proj", -1), (15, "x2T", -1)]

AT = {name: at for at, name, _ in SHARED}
OFFSET = {name: d for _, name, d in SHARED}


class Round:

    def __init__(self, i, c):
        self.i, self.c = i, c
        self.loop = not isinstance(i, int)
        self.u = None if self.loop else 2 * i + c

    def lin(self, per, add):
        return 2 * per * self.i + (per * self.c + add)

    def par(self, d=0):
        return (self.c + d) % 2

    def twos(self, d, per, add=0):
        return per * self.i + (per * ((self.c + d) // 2 + 1) + add)

    def has(self, d):
        return self.loop or 0 <= self.u + d < BLOCKS

    def has_pair(self, s, d=0):
        return self.loop or 0 <= STEPS * self.u + s + d < STEPS * BLOCKS

    def chunk(self, s, lag):
        if (s - lag) % 2 or not self.has_pair(s, -lag):
            return None
        return (0 if s >= lag else -1), (s - lag) % STEPS // 2

    def upto(self, step, back=0):
        def count(u):
            return sum(1 for r in range(FIRST, u + 1) for at, _, d in SHARED
                       if 0 <= r + d < BLOCKS and (r < u or at <= step))
        if not self.loop:
            return count(self.u - back)
        per = len(SHARED)
        return self.lin(per, count(LOOP_FROM) - per * LOOP_FROM - per * back)

    def shared(self, name, back=0):
        return self.upto(AT[name], back)


def need(eng, sem, value):
    if isinstance(value, int) and value <= 0:
        return
    eng.wait_ge(sem, value)


def rounds(eng, body):
    for u in range(FIRST, LOOP_FROM):
        body(Round(u // 2, u % 2))
    with eng.Fori((LOOP_FROM - 1) // 2, LOOP_TO // 2) as i:
        body(Round(i, 1))
        body(Round(i, 2))
    for u in range(LOOP_TO + 1, LAST + 1):
        body(Round(u // 2, u % 2))


def graph_transformer_layer(nc, x, adjT, wqT, bq, wkT, bk, wvT, bv, woT, bo, gamma, beta,
                            wg, bg, w1, b1T, w2, b2, out):
    ctx = ExitStack()
    with ctx:
        def sb(name, shape, dt=F32):
            return ctx.enter_context(nc.sbuf_tensor(name, shape, dt))

        def sem(name):
            return ctx.enter_context(nc.semaphore(name))

        def sem2(name):
            return [sem(f"{name}_{k}") for k in range(2)]

        def by_block(ap):
            return ap.rearrange("(v t p) d -> v p t d", t=TILES, p=P)

        x_blocks = by_block(x.rearrange("b n d -> (b n) d"))
        out_blocks = by_block(out.rearrange("b n d -> (b n) d"))
        scratch = nc.dram_tensor("xn_plus_bo_scratch", (BLOCKS, P, TILES, D), F32).ap()

        ident = sb("ident", [P, P])
        top = sb("top", [P, CHUNKS, SEQ])
        top_i = top[:].bitcast(I32)
        w_hi = sb("w_hi", [P, 4, D], F32R)
        w_lo = sb("w_lo", [P, 4, D], F32R)
        wg_hi_lo = sb("wg_hi_lo", [P, 2, EXPERTS], F32R)
        w1_hi = sb("w1_hi", [P, SLICES * P], F32R)
        w1_lo = sb("w1_lo", [P, SLICES * P], F32R)
        w2_sb = sb("w2_sb", [P, SLICES, D])
        b2_sb = sb("b2_sb", [EXPERTS, D])
        b1_sb = sb("b1_sb", [P, SLICES])
        bq_sb = sb("bq_sb", [P, 1])
        bk_sb = sb("bk_sb", [P, 1])
        rows = sb("rows", [P, 4, D])
        bv_row, bo_row, gamma_row, beta_row = (rows[:, k:k + 1, :].to_broadcast([P, TILES, D]) for k in range(4))
        bg_row = sb("bg_row", [P, 1, EXPERTS])
        expert_no = sb("expert_no", [P, 1, EXPERTS])
        minus_half = sb("minus_half", [P, TILES])

        k_stack = sb("k_stack", [P, HEADS, SEQ], F32R)
        q_stack = [sb(f"q_stack{k}", [P, HEADS, BLOCK], F32R) for k in range(2)]
        v_sb = sb("v_sb", [P, CHUNKS, D])
        ones = sb("ones", [P, DH])
        probs = sb("probs", [P, E_RING, 2, BLOCK])
        ctx_part = sb("ctx_part", [P, 2, SQUARES, DH])
        z_part = sb("z_part", [P, SQUARES, DH])
        z_inv = sb("z_inv", [P, SQUARES, 1])
        ctx_sum = sb("ctx_sum", [P, 2, SQUARES, DH])

        x_in = sb("x_in", [P, TILES, D])
        xn = sb("xn", [P, TILES, D])
        xnbo = sb("xnbo", [P, TILES, D])
        xnT_hi = sb("xnT_hi", [P, BLOCK], F32R)
        xnT_lo = sb("xnT_lo", [P, BLOCK], F32R)
        q_hi = sb("q_hi", [P, BLOCK], F32R)
        q_lo = sb("q_lo", [P, BLOCK], F32R)
        k_hi = [sb(f"k_hi{k}", [P, BLOCK], F32R) for k in range(2)]
        k_lo = [sb(f"k_lo{k}", [P, BLOCK], F32R) for k in range(2)]
        v_new = [sb(f"v_new{k}", [P, HALF, D]) for k in range(2)]

        ctxT = sb("ctxT", [P, BLOCK])
        ctxT_hi = sb("ctxT_hi", [P, BLOCK], F32R)
        ctxT_lo = sb("ctxT_lo", [P, BLOCK], F32R)
        x_post = sb("x_post", [P, TILES, D])
        xnbo_post = sb("xnbo_post", [P, TILES, D])
        res = sb("res", [P, TILES, D])
        x2 = sb("x2", [P, TILES, D])
        xn2 = sb("xn2", [P, TILES, D])
        xn2T_hi = [sb(f"xn2T_hi{k}", [P, BLOCK], F32R) for k in range(2)]
        xn2T_lo = [sb(f"xn2T_lo{k}", [P, BLOCK], F32R) for k in range(2)]

        gates = sb("gates", [P, TILES, EXPERTS])
        best = sb("best", [P, TILES, 8])
        best_at = sb("best_at", [P, TILES, 8], U32)
        is_second = sb("is_second", [P, TILES, EXPERTS])
        gate_lo = sb("gate_lo", [P, TILES, EXPERTS])
        chosen = sb("chosen", [P, 2, TILES, EXPERTS])
        chosenT = sb("chosenT", [EXPERTS, BLOCK])
        hidden = sb("hidden", [P, BURST, BLOCK])
        y_part = sb("y_part", [P, 2, TILES, D])
        y_sum = sb("y_sum", [P, 2, TILES, D])
        primed = sb("primed", [P, 1])

        def bank(name):
            return ctx.enter_context(nc.psum_tensor(name, [P, BLOCK], F32))

        scores_ps = [bank(f"scores_ps{k}") for k in range(2)]
        ctx_ps = bank("ctx_ps")
        z_ps = bank("z_ps")
        y_ps = bank("y_ps")
        shared_ps = bank("shared_ps")
        hidden_ps = [bank("hidden_ps0"), bank("hidden_ps1"), shared_ps]
        expert_ps = [hidden_ps[0], hidden_ps[1], y_ps]

        consts_loaded = sem("consts_loaded")
        adj_loaded = sem("adj_loaded")
        ident_zeroed = sem("ident_zeroed")
        passed = sem("passed")
        pool_consts = sem("pool_consts")
        split_hi = sem("split_hi")
        weights_split = sem("weights_split")
        top_raw = sem("top_raw")
        top_ready = sem("top_ready")

        score_ready = sem("score_ready")
        exp_done = sem("exp_done")
        probs_ready = sem("probs_ready")
        ctx_ready = sem("ctx_ready")
        ctx_turned = sem("ctx_turned")
        z_inverted = sem("z_inverted")
        ctx_scaled = sem("ctx_scaled")
        ctx_added = sem("ctx_added")
        ctxT_ready = sem("ctxT_ready")
        ctxT_split = sem("ctxT_split")

        shared_filled = sem("shared_filled")
        shared_drained = sem("shared_drained")
        hi_ready = {n: sem(f"hi_ready_{n}") for n in ("xnT", "q", "k", "ctxT", "x2T")}

        x_loaded = sem("x_loaded")
        post_loaded = sem2("post_loaded")
        xnbo_stored = sem2("xnbo_stored")
        q_copied = sem("q_copied")
        k_copied = sem2("k_copied")
        v_copied = sem2("v_copied")
        y_stored = sem2("y_stored")

        ln = {}
        for n in ("first", "second", "third"):
            ln[n] = dict(stats=sb(f"ln_stats_{n}", [P, TILES, 6]), mv=sb(f"ln_mv_{n}", [P, TILES, 2]),
                         rstd=sb(f"ln_rstd_{n}", [P, TILES]), s_stats=sem(f"ln_stats_ready_{n}"),
                         s_mv=sem(f"ln_mv_ready_{n}"), s_eps=sem(f"ln_eps_added_{n}"),
                         s_rstd=sem(f"ln_rstd_ready_{n}"), s_out=sem(f"ln_out_ready_{n}"))

        xnbo_ready = sem("xnbo_ready")
        x_beta_ready = sem("x_beta_ready")
        res_ready = sem("res_ready")
        res_scaled = sem("res_scaled")
        x2_ready = sem("x2_ready")

        gates_ready = sem("gates_ready")
        gate_lo_ready = sem("gate_lo_ready")
        best_ready = sem("best_ready")
        best_at_ready = sem("best_at_ready")
        ranks_ready = sem("ranks_ready")
        chosen_ready = sem("chosen_ready")

        hidden_pre = sem("hidden_pre")
        hidden_ready = sem("hidden_ready")
        hidden_used = sem("hidden_used")
        table_primed = sem("table_primed")
        y_masked = sem("y_masked")
        y_added = sem("y_added")

        def need_apart(eng, sem_, value):
            need(eng, sem_, value)
            eng.sem_inc(passed, 1)

        W_Q, W_K, W_V, W_O = range(4)
        KEYS = HALF * P

        block = ctx.enter_context(nc.Block())

        @block.sync
        def _(sp):
            def load(dst, src):
                sp.dma_start(dst, src).then_inc(consts_loaded, 16)

            def row(ap, n):
                return ap.rearrange("(a n) -> a n", a=1).to_broadcast([P, n])

            stage = probs[:].rearrange("p a b c -> p (a b c)")
            for k, w in enumerate((wqT, wkT, wvT, woT)):
                load(stage[:, 2048 + k * D:2048 + (k + 1) * D], w)
            for k, b in enumerate((bv, bo, gamma, beta)):
                load(rows[:, k, :], row(b, D))
            load(bg_row[:, 0, :], row(bg, EXPERTS))
            load(bq_sb[:], bq.rearrange("(p a) -> p a", a=1))
            load(bk_sb[:], bk.rearrange("(p a) -> p a", a=1))
            load(stage[:, 2560:2560 + EXPERTS], wg)
            load(stage[:, 0:2048].rearrange("p (e h) -> p e h", e=EXPERTS), w1.rearrange("e d h -> d e h"))
            load(b1_sb[:], b1T)
            load(b2_sb[:], b2)
            load(w2_sb[:].rearrange("p (e k) d -> p e k d", e=EXPERTS), w2.rearrange("e (k p) d -> p e k d", p=P))
            for c in range(CHUNKS):
                sp.dma_start(top_i[:, c, :], adjT[c * P:(c + 1) * P, :]).then_inc(adj_loaded, 16)

            def body(u):
                copy_q = u.has(1)
                if copy_q:
                    v = u.par(1)
                    need_apart(sp, shared_drained, u.shared("q", back=1))
                    need(sp, score_ready, u.lin(2 * STEPS, 0) if u.has(-1) else 0)
                    for h in range(HEADS):
                        rows_of = slice(DH * h, DH * (h + 1))
                        for g, part in enumerate((q_hi, q_hi, q_lo, q_lo)):
                            sp.dma_start(q_stack[v][DH * g:DH * (g + 1), h, :].bitcast(F32),
                                         part[rows_of, :].bitcast(F32)).then_inc(q_copied, 16)

                def copy_kv():
                    v = u.par(1)
                    step = 0 if v else HALF * 2
                    need_apart(sp, shared_drained, u.shared("v", back=1))
                    need(sp, score_ready, u.lin(2 * STEPS, 2 * step) if u.has(-1) else 0)
                    for h in range(HEADS):
                        rows_of = slice(DH * h, DH * (h + 1))
                        for g, part in enumerate((k_hi, k_lo, k_hi, k_lo)):
                            sp.dma_start(k_stack[DH * g:DH * (g + 1), h, KEYS * v:KEYS * (v + 1)].bitcast(F32),
                                         part[v][rows_of, :].bitcast(F32)).then_inc(k_copied[v], 16)
                    need(sp, ctx_ready, u.lin(CHUNKS, step // 2) if u.has(-1) else 0)
                    sp.dma_start(v_sb[:, HALF * v:HALF * (v + 1), :], v_new[v][:]).then_inc(v_copied[v], 16)

                if u.has(1) and u.par(1):
                    copy_kv()
                if u.has(3):
                    need(sp, ln["first"]["s_out"], u.lin(1, 3))
                    sp.dma_start(x_in[:], x_blocks[u.lin(1, 3)]).then_inc(x_loaded, 16)
                if u.has(-1):
                    need(sp, x2_ready, u.lin(1, -1))
                    need(sp, xnbo_stored[u.par(-1)], u.twos(-1, 16))
                    sp.dma_start(x_post[:], x_blocks[u.lin(1, -1)]).then_inc(post_loaded[u.par(-1)], 16)
                    sp.dma_start(xnbo_post[:], scratch[u.lin(1, -1)]).then_inc(post_loaded[u.par(-1)], 16)
                if u.has(1) and not u.par(1):
                    copy_kv()
                if u.has(-3):
                    need(sp, y_added, u.lin(EXPERTS, -2 * EXPERTS))
                    sp.dma_start(out_blocks[u.lin(1, -3)], y_sum[:, u.par(-3), :, :]).then_inc(y_stored[u.par(-3)], 16)
                if u.has(3):
                    need(sp, xnbo_ready, u.lin(1, 4))
                    sp.dma_start(scratch[u.lin(1, 3)], xnbo[:]).then_inc(xnbo_stored[u.par(3)], 16)

            rounds(sp, body)
            for k in range(2):
                sp.wait_ge(y_stored[k], 16 * BLOCKS // 2)
                sp.wait_ge(xnbo_stored[k], 16 * BLOCKS // 2)

        @block.tensor
        def _(pe):
            def fill(name, u, emit):
                need(pe, shared_drained, u.shared(name) + (-1))
                if name in ("xnT", "gate") and u.has(-3):
                    need(pe, hidden_ready, u.lin(SLICES, -2 * SLICES))
                if name in ("proj", "x2T") and u.has(-2):
                    need(pe, hidden_ready, u.lin(SLICES, BURST - 2 * SLICES))
                emit().then_inc(shared_filled, 1)

            def transposes(src):
                for t in range(TILES):
                    last = pe.transpose(shared_ps[:, t * P:(t + 1) * P], src[:, t, :], ident[:])
                return last

            def three(dst, l_hi, l_lo, r_hi, r_lo):
                pe.matmul(dst, l_hi, r_hi, start=True, stop=False)
                pe.matmul(dst, l_hi, r_lo, start=False, stop=False)
                return pe.matmul(dst, l_lo, r_hi, start=False, stop=True)

            def shared_use(name, u):
                if name == "xnT":
                    need(pe, ln["first"]["s_out"], u.lin(1, 3))
                    fill(name, u, lambda: transposes(xn))
                elif name in ("q", "k"):
                    w = W_Q if name == "q" else W_K
                    if name == "k":
                        need(pe, weights_split, 1)
                    fill(name, u, lambda: three(shared_ps[:], w_hi[:, w, :], w_lo[:, w, :], xnT_hi[:], xnT_lo[:]))
                elif name == "v":
                    def emit():
                        for t in range(TILES):
                            cols = slice(t * P, (t + 1) * P)
                            last = three(shared_ps[:, cols], xnT_hi[:, cols], xnT_lo[:, cols],
                                         w_hi[:, W_V, :], w_lo[:, W_V, :])
                        return last
                    fill(name, u, emit)
                elif name == "proj":
                    need(pe, ctxT_split, u.lin(1, 0))

                    def emit():
                        for t in range(TILES):
                            cols = slice(t * P, (t + 1) * P)
                            last = three(shared_ps[:, cols], ctxT_hi[:, cols], ctxT_lo[:, cols],
                                         w_hi[:, W_O, :], w_lo[:, W_O, :])
                        return last
                    fill(name, u, emit)
                elif name == "x2T":
                    need(pe, ln["third"]["s_out"], u.lin(1, 0))
                    fill(name, u, lambda: transposes(xn2))
                elif name == "gate":
                    def emit():
                        b = u.par(-2)
                        for t in range(TILES):
                            cols = slice(t * P, (t + 1) * P)
                            dst = shared_ps[:, 2 * t * EXPERTS:2 * (t + 1) * EXPERTS]
                            both = wg_hi_lo[:].rearrange("p a e -> p (a e)")
                            pe.matmul(dst, xn2T_hi[b][:, cols], both, start=True, stop=False)
                            last = pe.matmul(dst, xn2T_lo[b][:, cols], both, start=False, stop=True)
                        return last
                    fill(name, u, emit)
                elif name == "maskT":
                    need(pe, chosen_ready, u.lin(1, -1))

                    def emit():
                        for t in range(TILES):
                            last = pe.transpose(shared_ps[0:EXPERTS, t * P:(t + 1) * P],
                                                chosen[:, u.par(-2), t, :], ident[:])
                        return last
                    fill(name, u, emit)
                elif name == "b2":
                    def emit():
                        for t in range(TILES):
                            last = pe.matmul(shared_ps[:, t * P:(t + 1) * P], chosenT[:, t * P:(t + 1) * P],
                                             b2_sb[:], start=True, stop=True)
                        return last
                    fill(name, u, emit)

            def scores(u, s, hh):
                h, j = 2 * (s % 2) + hh, s // 2
                if hh == 0 and s == 0:
                    pe.wait_ge(q_copied, u.lin(256, 256))
                    if u.par() == 0:
                        pe.wait_ge(k_copied[0], u.twos(0, 256))
                if hh == 0 and s == 2 * HALF and u.par() == 0:
                    pe.wait_ge(k_copied[1], u.twos(1, 256))
                need(pe, exp_done, u.lin(2 * STEPS, 2 * s - 1 + hh))
                pe.matmul(scores_ps[hh][:], k_stack[:, h, j * P:(j + 1) * P], q_stack[u.par()][:, h, :],
                          start=True, stop=True).then_inc(score_ready, 1)

            def context(u, rnd, j):
                if j == 0 and u.par(rnd) == 0:
                    pe.wait_ge(v_copied[0], u.twos(rnd, 16))
                if j == HALF and u.par(rnd) == 0:
                    pe.wait_ge(v_copied[1], u.twos(rnd + 1, 16))
                need(pe, probs_ready, u.lin(STEPS, STEPS * rnd + 2 * j + 2))
                need(pe, ctx_turned, u.lin(CHUNKS, CHUNKS * rnd + j))
                for dst, weights in ((ctx_ps, v_sb), (z_ps, None)):
                    for h in range(HEADS):
                        rows_of = slice(DH * h, DH * (h + 1))
                        left = ones[:] if weights is None else weights[:, j, rows_of]
                        last = pe.matmul(dst[rows_of, :], left, probs[:, (2 * j + h // 2) % E_RING, h % 2, :],
                                         start=True, stop=True)
                last.then_inc(ctx_ready, 1)

            def first_products(u, k0):
                b = u.par(-2)
                if k0 == 0:
                    need(pe, shared_drained, u.shared("x2T", back=1))
                for k in range(BURST):
                    if BURST_BEFORE[k] is not None:
                        need(pe, hidden_ready, u.lin(SLICES, k0 + BURST_BEFORE[k] + 1 - 2 * SLICES))
                    elif BURST_BANK[k] == 2:
                        need(pe, shared_drained, u.upto(BURST - 1 if k0 == 0 else STEPS - 1))
                    else:
                        need(pe, y_masked, u.lin(EXPERTS, k0 // 2 - BURST_BANK[k] - 1 - 2 * EXPERTS))
                    cols = slice((k0 + k) * P, (k0 + k + 1) * P)
                    three(hidden_ps[BURST_BANK[k]][:], w1_hi[:, cols], w1_lo[:, cols], xn2T_hi[b][:], xn2T_lo[b][:])\
                        .then_inc(hidden_pre, 1)

            def second_product(u, k, back):
                need(pe, hidden_ready, u.lin(SLICES, k + 1 - back * SLICES))
                e = k // 2
                ps = expert_ps[Y_BANK[e]]
                if k % 2 == 0 and e % 4 >= 2:
                    need(pe, y_masked, u.lin(EXPERTS, (e - 1 if e % 4 == 2 else e - 3) - back * EXPERTS))
                elif k % 2 == 0:
                    need(pe, hidden_ready, u.lin(SLICES, (k // BURST + 1) * BURST - back * SLICES))
                for t in range(TILES):
                    last = pe.matmul(ps[:, t * P:(t + 1) * P], hidden[:, k % BURST, t * P:(t + 1) * P],
                                     w2_sb[:, k, :], start=(k % 2 == 0 and t == 0),
                                     stop=(k % 2 == 1 and t == TILES - 1), skip_group_check=True)
                last.then_inc(hidden_used, 1)

            pe.wait_ge(pool_consts, 2)

            def body(u):
                for s in range(STEPS):
                    if u.has_pair(s):
                        scores(u, s, 0)
                        scores(u, s, 1)
                    due = u.chunk(s, CONTEXT_LAG)
                    if due is not None:
                        context(u, *due)
                    if s < BURST and u.has(-3):
                        second_product(u, BURST + s, 3)
                    if s >= BURST and u.has(-2):
                        second_product(u, s - BURST, 2)
                    for at, name, d in SHARED:
                        if at == s and u.has(d):
                            shared_use(name, u)
                    if s in (BURST - 1, STEPS - 1) and u.has(-2):
                        first_products(u, 0 if s < BURST else BURST)

            rounds(pe, body)

        @block.scalar
        def _(act):
            act.wait_ge(consts_loaded, 16 * 16)

            def hi_part(u, name, dst, free, bias=None):
                need(act, shared_filled, u.shared(name))
                for s_, v_ in free:
                    need(act, s_, v_)
                if bias is None:
                    ins = nc.scalar.activation(dst, shared_ps[:], ACT.Copy)
                else:
                    ins = nc.scalar.activation(dst, shared_ps[:], ACT.Identity, bias=bias)
                ins.then_inc(hi_ready[name], 1)

            def gelu(u, k0):
                for k in range(k0, k0 + BURST):
                    need(act, hidden_pre, u.lin(SLICES, k + 1 - 2 * SLICES))
                    need(act, hidden_used, u.lin(SLICES, k + 1 - BURST - 2 * SLICES))
                    nc.scalar.activation(hidden[:, k % BURST, :], hidden_ps[BURST_BANK[k % BURST]][:], ACT.Gelu,
                                         bias=b1_sb[:, k:k + 1]).then_inc(hidden_ready, 1)

            def prime_gelu(u, k0):
                n = u.lin(2, (1 if k0 == 0 else 2) - 4)
                need(act, table_primed, n - 1 if isinstance(n, int) else n + (-1))
                nc.scalar.activation(primed[:], b1_sb[:, 0:1], ACT.Gelu).then_inc(table_primed, 1)

            def mask_expert(u, e, back):
                need(act, hidden_used, u.lin(SLICES, 2 * e + 2 - back * SLICES))
                need(act, y_added, u.lin(EXPERTS, e - 1 - back * EXPERTS))
                need(act, chosen_ready, u.lin(1, 1 - back))
                for t in range(TILES):
                    last = nc.scalar.activation(y_part[:, e % 2, t, :],
                                                expert_ps[Y_BANK[e]][:, t * P:(t + 1) * P], ACT.Copy,
                                                scale=chosen[:, u.par(-back), t, e:e + 1])
                last.then_inc(y_masked, 1)

            def body(u):
                for s in range(STEPS):
                    if u.has_pair(s):
                        for hh in range(2):
                            need(act, score_ready, u.lin(2 * STEPS, 2 * s + hh + 1))
                            if hh == 0:
                                need(act, ctx_ready, u.lin(CHUNKS, (s - E_RING) // 2 + 1))
                            nc.scalar.activation(probs[:, s % E_RING, hh, :], scores_ps[hh][:], ACT.Exp,
                                                 scale=SCORE_SCALE).then_inc(exp_done, 1)
                    if s % 2 == 0 and s <= 8 and u.has(-3):
                        mask_expert(u, 3 + s // 2, 3)
                    if s % 2 == 0 and s >= 10 and u.has(-2):
                        mask_expert(u, (s - 10) // 2, 2)
                    if s in (BURST - 1, STEPS - 1) and u.has(-2):
                        prime_gelu(u, 0 if s < BURST else BURST)
                    if s == 5 and u.has(-1):
                        if u.has(-2):
                            need(act, shared_filled, u.shared("proj", back=1))
                        need(act, ctxT_ready, u.lin(1, 0))
                        nc.scalar.activation(ctxT_hi[:], ctxT[:], ACT.Copy).then_inc(hi_ready["ctxT"], 1)
                    for at, name, d in SHARED:
                        if at != s or not u.has(d):
                            continue
                        b = u.par(d)
                        if name == "xnT":
                            hi_part(u, name, xnT_hi[:], [(shared_filled, u.shared("q", back=1) if u.has(1) else 0)])
                        elif name == "q":
                            hi_part(u, name, q_hi[:], [(q_copied, u.lin(256, 256 * d))], bq_sb[:, 0:1])
                        elif name == "k":
                            hi_part(u, name, k_hi[b][:], [(k_copied[b], u.twos(d - 2, 256))], bk_sb[:, 0:1])
                        elif name == "x2T":
                            hi_part(u, name, xn2T_hi[b][:], [(hidden_pre, u.lin(SLICES, -2 * SLICES))])
                    if s in (BURST - 1, STEPS - 1) and u.has(-2):
                        gelu(u, 0 if s < BURST else BURST)

            rounds(act, body)

        @block.vector
        def _(dve):
            def filled(u, name):
                need(dve, shared_filled, u.shared(name))

            def lo_part(u, name, dst, hi, bias=None):
                need(dve, hi_ready[name], u.lin(1, OFFSET[name] + 1))
                if bias is None:
                    ins = dve.tensor_tensor(dst, shared_ps[:], hi.bitcast(F32), ALU.subtract)
                else:
                    ins = dve.scalar_tensor_tensor(out=dst, in0=shared_ps[:], scalar=bias, in1=hi.bitcast(F32),
                                                   op0=ALU.add, op1=ALU.subtract)
                ins.then_inc(shared_drained, 1)

            def statistics(l, src, count):
                for t in range(TILES):
                    last = dve.bn_stats(l["stats"][:, t, :], src[:, t, :])
                last.then_inc(l["s_stats"], 1)
                need_apart(dve, l["s_stats"], count)
                for t in range(TILES):
                    last = dve.bn_aggr(l["mv"][:, t, :], l["stats"][:, t, :])
                last.then_inc(l["s_mv"], 1)

            def normalise(l, dst, src, count):
                dve.wait_ge(l["s_rstd"], count)
                for t in range(TILES):
                    last = dve.tensor_scalar(dst[:, t, :], src[:, t, :], l["mv"][:, t, 0:1], l["rstd"][:, t:t + 1],
                                             ALU.subtract, ALU.mult)
                last.then_inc(l["s_out"], 1)

            stage = probs[:].rearrange("p a b c -> p (a b c)")
            dve.wait_ge(consts_loaded, 16 * 16)
            parts = [(w_hi[:].rearrange("p a b -> p (a b)"), w_lo[:].rearrange("p a b -> p (a b)"), stage[:, 2048:2560]),
                     (wg_hi_lo[:, 0, :], wg_hi_lo[:, 1, :], stage[:, 2560:2560 + EXPERTS]),
                     (w1_hi[:], w1_lo[:], stage[:, 0:2048])]
            for hi, lo, src in parts:
                dve.tensor_copy(hi, src).then_inc(split_hi, 1)
            for n, (hi, lo, src) in enumerate(parts):
                dve.wait_ge(split_hi, n + 1)
                dve.tensor_tensor(lo, src, hi.bitcast(F32), ALU.subtract).then_inc(weights_split, 1)
            def mask_chunk(j):
                dve.wait_ge(adj_loaded, 16 * CHUNKS)
                dve.tensor_scalar(top[:, j, :], top_i[:, j, :], 0.0, P_HIGH, ALU.not_equal, ALU.mult).then_inc(top_raw, 1)
                dve.wait_ge(top_raw, j + 1)
                dve.tensor_scalar(top[:, j, :], top[:, j, :], P_LOW, None, ALU.max).then_inc(top_ready, 1)

            def probabilities(u, s):
                back = s - 1
                ps, nb = back % STEPS, u.par(0 if back >= 0 else -1)
                j = ps // 2
                if not u.loop and u.u <= 1:
                    dve.wait_ge(top_ready, j + 1)
                need(dve, exp_done, u.lin(2 * STEPS, 2 * back + 2))
                e = probs[:, ps % E_RING, :, :]
                bound = top[:, j:j + 1, nb * BLOCK:(nb + 1) * BLOCK].to_broadcast([P, 2, BLOCK])
                dve.scalar_tensor_tensor(out=e, in0=e, scalar=P_LOW, in1=bound, op0=ALU.max, op1=ALU.min)\
                    .then_inc(probs_ready, 1)

            def turn(u, rnd, j):
                need(dve, ctx_ready, u.lin(CHUNKS, CHUNKS * rnd + j + 1))
                if j != 2:
                    need(dve, ctx_added, u.lin(CHUNKS - 1, (CHUNKS - 1) * rnd + max(j - 2, 0) if j else
                                               (CHUNKS - 1) * (rnd - 1) + CHUNKS - 2))
                dve.transpose(ctx_part[:, j % 2, :, :].rearrange("p a b -> p (a b)"), ctx_ps[:])
                dve.transpose(z_part[:].rearrange("p a b -> p (a b)"), z_ps[:]).then_inc(ctx_turned, 1)

            def invert_sums(u, rnd, j):
                need(dve, ctx_turned, u.lin(CHUNKS, CHUNKS * rnd + j + 1))
                dve.reciprocal(z_inv[:], z_part[:, :, 0:1]).then_inc(z_inverted, 1)

            def scale(u, rnd, j):
                if j == 0:
                    need(dve, ctxT_ready, u.lin(1, rnd - 1))
                    dst = ctx_sum[:, u.par(rnd), :, :]
                else:
                    dst = ctx_part[:, j % 2, :, :]
                need(dve, z_inverted, u.lin(CHUNKS, CHUNKS * rnd + j + 1))
                dve.tensor_tensor(dst, ctx_part[:, j % 2, :, :], z_inv[:].to_broadcast([P, SQUARES, DH]), ALU.mult)\
                    .then_inc(ctx_scaled, 1)

            def drain(u, name):
                ps3 = shared_ps[:].rearrange("p (t d) -> p t d", t=TILES)
                if name == "xnT":
                    lo_part(u, name, xnT_lo[:], xnT_hi[:])
                elif name == "q":
                    lo_part(u, name, q_lo[:], q_hi[:], bq_sb[:, 0:1])
                elif name == "k":
                    b = u.par(2)
                    lo_part(u, name, k_lo[b][:], k_hi[b][:], bk_sb[:, 0:1])
                elif name == "v":
                    b = u.par(2)
                    filled(u, name)
                    need(dve, v_copied[b], u.twos(0, 16))
                    dve.tensor_tensor(v_new[b][:], ps3, bv_row, ALU.add).then_inc(shared_drained, 1)
                elif name == "proj":
                    filled(u, name)
                    need(dve, post_loaded[u.par(-1)], u.twos(-1, 32))
                    need(dve, x2_ready, u.lin(1, -1))
                    dve.tensor_tensor(res[:], ps3, xnbo_post[:], ALU.add).then_inc(shared_drained, 1)
                    dve.wait_ge(shared_drained, u.shared(name))
                    statistics(ln["second"], res, u.lin(1, 0))
                elif name == "x2T":
                    b = u.par(-1)
                    lo_part(u, name, xn2T_lo[b][:], xn2T_hi[b][:])
                elif name == "gate":
                    filled(u, name)
                    n = u.lin(1, -1)
                    g = shared_ps[:, 0:2 * TILES * EXPERTS].rearrange("p (t a e) -> p t a e", a=2, e=EXPERTS)
                    dve.tensor_tensor(gate_lo[:], g[:, :, 1, :], bg_row[:].to_broadcast([P, TILES, EXPERTS]), ALU.add)\
                        .then_inc(gate_lo_ready, 1)
                    need(dve, gate_lo_ready, n)
                    dve.tensor_tensor(gates[:], g[:, :, 0, :], gate_lo[:], ALU.add).then_inc(shared_drained, 1)
                    need_apart(dve, shared_drained, u.shared(name))
                    for t in range(TILES):
                        last = dve.max(best[:, t, :], gates[:, t, :])
                    last.then_inc(best_ready, 1)
                    need_apart(dve, best_ready, n)
                    for t in range(TILES):
                        last = dve.max_index(best_at[:, t, :], best[:, t, :], gates[:, t, :])
                    last.then_inc(best_at_ready, 1)
                    dve.wait_ge(best_at_ready, n)
                    no = expert_no[:].to_broadcast([P, TILES, EXPERTS])
                    one, two = (best_at[:, :, k:k + 1].to_broadcast([P, TILES, EXPERTS]) for k in range(2))
                    c = chosen[:, u.par(-2), :, :]
                    dve.tensor_tensor(c, no, one, ALU.is_equal)
                    dve.tensor_tensor(is_second[:], no, two, ALU.is_equal).then_inc(ranks_ready, 1)
                    dve.wait_ge(ranks_ready, n)
                    dve.tensor_tensor(c, c, is_second[:], ALU.add).then_inc(chosen_ready, 1)
                elif name == "maskT":
                    filled(u, name)
                    dve.tensor_copy(chosenT[:], shared_ps[0:EXPERTS, :]).then_inc(shared_drained, 1)
                elif name == "b2":
                    filled(u, name)
                    need(dve, y_stored[u.par(-2)], u.twos(-4, 16))
                    dve.tensor_tensor(y_sum[:, u.par(-2), :, :], ps3, x2[:], ALU.add).then_inc(shared_drained, 1)

            dve.wait_ge(pool_consts, 2)

            def body(u):
                for s in range(STEPS):
                    if not u.loop and u.u == 0 and s % 2 == 0:
                        mask_chunk(s // 2)
                    if u.has_pair(s, -1):
                        probabilities(u, s)
                    for at, name, d in SHARED:
                        if at == s - 1 and u.has(d):
                            drain(u, name)
                        if at == STEPS - 1 and s == 0 and u.has(d - 1):
                            drain(previous(u), name)
                    due = u.chunk(s, TURN_LAG)
                    if due is not None:
                        turn(u, *due)
                        invert_sums(u, *due)
                    due = u.chunk(s, SCALE_LAG)
                    if due is not None:
                        scale(u, *due)
                    if s == 5 and u.has(-1):
                        need(dve, ctxT_split, u.lin(1, -1))
                        need(dve, ctx_added, u.lin(CHUNKS - 1, 0))
                        dve.transpose(ctxT[:], ctx_sum[:, u.par(-1), :, :].rearrange("p a b -> p (a b)"))\
                            .then_inc(ctxT_ready, 1)
                    if s == 7 and u.has(-1):
                        need(dve, hi_ready["ctxT"], u.lin(1, 0))
                        dve.tensor_tensor(ctxT_lo[:], ctxT[:], ctxT_hi[:].bitcast(F32), ALU.subtract)\
                            .then_inc(ctxT_split, 1)
                    if s == 11 and u.has(-1):
                        normalise(ln["second"], res, res, u.lin(1, 0))
                    if s == 12 and u.has(3):
                        need(dve, x_loaded, u.lin(16, 64))
                        statistics(ln["first"], x_in, u.lin(1, 4))
                    if s == 13 and u.has(-1):
                        need(dve, x2_ready, u.lin(1, 0))
                        statistics(ln["third"], x2, u.lin(1, 0))
                    if s == 14 and u.has(-1):
                        need(dve, shared_filled, u.shared("x2T", back=1) if u.has(-2) else 0)
                        normalise(ln["third"], xn2, x2, u.lin(1, 0))
                    if s == 15 and u.has(3):
                        need(dve, shared_filled, u.shared("xnT") if u.has(2) else 0)
                        need(dve, xnbo_ready, u.lin(1, 3))
                        normalise(ln["first"], xn, x_in, u.lin(1, 4))

            def previous(u):
                return Round(u.i, u.c - 1)

            rounds(dve, body)

        @block.gpsimd
        def _(pool):
            nc.gpsimd.memset(ident[:], 0.0).then_inc(ident_zeroed, 1)
            nc.gpsimd.memset(minus_half[:], -0.5)
            nc.gpsimd.memset(ones[:], 1.0)
            pool.wait_ge(ident_zeroed, 1)
            nc.gpsimd.affine_select(out=ident[:], in_=ident[:], compare_op=ALU.not_equal, fill=1.0, base=0,
                                    pattern=[[-1, P]], channel_multiplier=1).then_inc(pool_consts, 1)
            for e in range(EXPERTS):
                last = nc.gpsimd.memset(expert_no[:, :, e:e + 1], float(e))
            last.then_inc(pool_consts, 1)
            pool.wait_ge(consts_loaded, 16 * 16)
            pool.wait_ge(pool_consts, 2)

            def root(l, count):
                need_apart(pool, l["s_mv"], count)
                nc.gpsimd.tensor_scalar(l["rstd"][:], l["mv"][:, :, 1], LN_EPS, None, ALU.add).then_inc(l["s_eps"], 1)
                pool.wait_ge(l["s_eps"], count)
                nc.gpsimd.tensor_tensor(l["rstd"][:], l["rstd"][:], minus_half[:], ALU.pow).then_inc(l["s_rstd"], 1)

            def add_context(u, rnd, j):
                need(pool, ctx_scaled, u.lin(CHUNKS, CHUNKS * rnd + j + 1))
                need(pool, ctx_added, u.lin(CHUNKS - 1, (CHUNKS - 1) * rnd + j - 1))
                dst = ctx_sum[:, u.par(rnd), :, :]
                nc.gpsimd.tensor_tensor(dst, dst, ctx_part[:, j % 2, :, :], ALU.add).then_inc(ctx_added, 1)

            def add_expert(u, e, back):
                need(pool, y_masked, u.lin(EXPERTS, e + 1 - back * EXPERTS))
                need(pool, y_added, u.lin(EXPERTS, e - back * EXPERTS))
                dst = y_sum[:, u.par(-back), :, :]
                nc.gpsimd.tensor_tensor(dst, dst, y_part[:, e % 2, :, :], ALU.add).then_inc(y_added, 1)

            def body(u):
                for s in range(STEPS):
                    due = u.chunk(s, SCALE_LAG)
                    if due is not None and due[1] > 0:
                        add_context(u, *due)
                    if s % 2 == 0 and s <= 8 and u.has(-3):
                        add_expert(u, 3 + s // 2, 3)
                    if s % 2 == 0 and s >= 10 and u.has(-2):
                        add_expert(u, (s - 10) // 2, 2)
                    if s == 5 and u.has(-1):
                        need(pool, post_loaded[u.par(-1)], u.twos(-1, 32))
                        nc.gpsimd.tensor_tensor(x_post[:], x_post[:], beta_row, ALU.add).then_inc(x_beta_ready, 1)
                    if s == 10 and u.has(-1):
                        root(ln["second"], u.lin(1, 0))
                    if s == 11 and u.has(-1):
                        need(pool, ln["second"]["s_out"], u.lin(1, 0))
                        nc.gpsimd.tensor_tensor(res[:], res[:], gamma_row, ALU.mult).then_inc(res_scaled, 1)
                        need(pool, res_scaled, u.lin(1, 0))
                        need(pool, x_beta_ready, u.lin(1, 0))
                        if u.has(-2):
                            need(pool, shared_drained, u.shared("b2"))
                        nc.gpsimd.tensor_tensor(x2[:], res[:], x_post[:], ALU.add).then_inc(x2_ready, 1)
                    if s == 12 and u.has(3):
                        root(ln["first"], u.lin(1, 4))
                    if s == 13 and u.has(-1):
                        root(ln["third"], u.lin(1, 0))
                    if s == 15 and u.has(3):
                        need(pool, ln["first"]["s_out"], u.lin(1, 4))
                        need(pool, xnbo_stored[u.par(2)], u.twos(2, 16))
                        nc.gpsimd.tensor_tensor(xnbo[:], xn[:], bo_row, ALU.add).then_inc(xnbo_ready, 1)

            rounds(pool, body)


def kernel(x, adj, L0_gnn_Wq, L0_gnn_bq, L0_gnn_Wk, L0_gnn_bk, L0_gnn_Wv, L0_gnn_bv, L0_gnn_Wo, L0_gnn_bo,
           L0_gnn_gamma, L0_gnn_beta, L0_ffn_Wg, L0_ffn_bg, L0_ffn_W1, L0_ffn_b1, L0_ffn_W2, L0_ffn_b2):
    import concourse.bacc as bacc
    from concourse.bass_utils import run_bass_kernel_spmd

    laid = dict(x=x, adjT=np.asarray(adj).T, wqT=np.asarray(L0_gnn_Wq).T, bq=L0_gnn_bq,
                wkT=np.asarray(L0_gnn_Wk).T, bk=L0_gnn_bk, wvT=np.asarray(L0_gnn_Wv).T, bv=L0_gnn_bv,
                woT=np.asarray(L0_gnn_Wo).T, bo=L0_gnn_bo, gamma=L0_gnn_gamma, beta=L0_gnn_beta,
                wg=L0_ffn_Wg, bg=L0_ffn_bg, w1=L0_ffn_W1,
                b1T=np.asarray(L0_ffn_b1).reshape(SLICES, P).T, w2=L0_ffn_W2, b2=L0_ffn_b2)
    nc = bacc.Bacc("TRN2", target_bir_lowering=False, num_devices=1)
    arrays, args = {}, []
    for name, value in laid.items():
        a = np.ascontiguousarray(value)
        arrays[f"in_{name}"] = a
        args.append(nc.dram_tensor(f"in_{name}", a.shape, mybir.dt.from_np(a.dtype), kind="ExternalInput").ap())
    out = nc.dram_tensor("out", (BATCH, SEQ, D), F32, kind="ExternalOutput").ap()
    graph_transformer_layer(nc, *args, out)
    results = run_bass_kernel_spmd(nc, [arrays], core_ids=[0])
    return results.results[0]["out"]
```

```python
from contextlib import ExitStack

import numpy as np

import concourse.bass as bass
from concourse import mybir

F32 = mybir.dt.float32
F32R = mybir.dt.float32r
I32 = mybir.dt.int32
U32 = mybir.dt.uint32
ALU = mybir.AluOpType
ACT = mybir.ActivationFunctionType

P = 128
BATCH, SEQ, D = 8, 1024, 128
HEADS, DH = 4, 32
EXPERTS, HIDDEN = 8, 256
BLOCK = 512
TILES = BLOCK // P
BLOCKS = BATCH * SEQ // BLOCK
CHUNKS = SEQ // P
STEPS = CHUNKS * HEADS // 2
SQUARES = BLOCK // DH
SLICES = EXPERTS * HIDDEN // P
BURST = SLICES // 2
HALF = TILES
E_RING = 4
LN_EPS = 1e-5
SCORE_SCALE = 1.0 / float(np.sqrt(DH))
P_LOW = float(np.exp(np.float32(-10.0)))
P_HIGH = float(np.exp(np.float32(10.0)))

CONTEXT_LAG, TURN_LAG = 3, 4
PART_RING = 4
BURST_BANK = (0, 1, 2, 0, 1, 2, 0, 1)
BURST_BEFORE = (None, None, None, 0, 1, 2, 3, 4)
Y_BANK = (0, 1, 0, 2) * 2
FIRST, LAST = -3, BLOCKS + 2
LOOP_FROM, LOOP_TO = 5, 12

SHARED = [(0, "xnT", 2), (1, "x2T", -2), (2, "k", 2), (3, "gate", -2), (4, "v", 2), (5, "maskT", -2),
          (6, "q", 2), (7, "proj", -1), (9, "b2", -2)]

AT = {name: at for at, name, _ in SHARED}
OFFSET = {name: d for _, name, d in SHARED}


class Round:

    def __init__(self, i, c):
        self.i, self.c = i, c
        self.loop = not isinstance(i, int)
        self.u = None if self.loop else 2 * i + c

    def lin(self, per, add):
        return 2 * per * self.i + (per * self.c + add)

    def par(self, d=0):
        return (self.c + d) % 2

    def twos(self, d, per, add=0):
        return per * self.i + (per * ((self.c + d) // 2 + 1) + add)

    def has(self, d):
        return self.loop or 0 <= self.u + d < BLOCKS

    def has_pair(self, s, d=0):
        return self.loop or 0 <= STEPS * self.u + s + d < STEPS * BLOCKS

    def chunk(self, s, lag):
        if (s - lag) % 2 or not self.has_pair(s, -lag):
            return None
        return (0 if s >= lag else -1), (s - lag) % STEPS // 2

    def next(self):
        return Round(self.i, self.c + 1)

    def previous(self):
        return Round(self.i, self.c - 1)

    def scored_early(self, s):
        return (s == BURST and self.has(-2)) or (s == 0 and self.has(-3))

    def upto(self, step, back=0):
        def count(u):
            return sum(1 for r in range(FIRST, u + 1) for at, _, d in SHARED
                       if 0 <= r + d < BLOCKS and (r < u or at <= step))
        if not self.loop:
            return count(self.u - back)
        per = len(SHARED)
        return self.lin(per, count(LOOP_FROM) - per * LOOP_FROM - per * back)

    def shared(self, name, back=0):
        return self.upto(AT[name], back)

def ln_steps(u):
    if u.loop or u.u > 1:
        return 8, 8, 8, 8
    if u.u >= 0:
        return 8, 9, 11, 13
    return 3, 3, 3, 3


def need(eng, sem, value):
    if isinstance(value, int) and value <= 0:
        return
    eng.wait_ge(sem, value)


def rounds(eng, body):
    for u in range(FIRST, LOOP_FROM):
        body(Round(u // 2, u % 2))
    with eng.Fori((LOOP_FROM - 1) // 2, LOOP_TO // 2) as i:
        body(Round(i, 1))
        body(Round(i, 2))
    for u in range(LOOP_TO + 1, LAST + 1):
        body(Round(u // 2, u % 2))


def graph_transformer_layer(nc, x, adjT, wqT, bq, wkT, bk, wvT, bv, woT, bo, gamma, beta,
                            wg, bg, w1, b1T, w2, b2, out):
    ctx = ExitStack()
    with ctx:
        def sb(name, shape, dt=F32):
            return ctx.enter_context(nc.sbuf_tensor(name, shape, dt))

        def sem(name):
            return ctx.enter_context(nc.semaphore(name))

        def sem2(name):
            return [sem(f"{name}_{k}") for k in range(2)]

        def by_block(ap):
            return ap.rearrange("(v t p) d -> v p t d", t=TILES, p=P)

        x_blocks = by_block(x.rearrange("b n d -> (b n) d"))
        out_blocks = by_block(out.rearrange("b n d -> (b n) d"))
        scratch = nc.dram_tensor("xn_plus_bo_scratch", (BLOCKS, P, TILES, D), F32).ap()

        q_scratch = nc.dram_tensor("q_scratch", (2, P, BLOCK), F32).ap()
        k_scratch = nc.dram_tensor("k_scratch", (2, P, BLOCK), F32).ap()

        ident = sb("ident", [P, P])
        top = sb("top", [P, CHUNKS, SEQ])
        top_i = top[:].bitcast(I32)
        w_hi = sb("w_hi", [P, 4, D], F32R)
        w_lo = sb("w_lo", [P, 4, D], F32R)
        wg_hi_lo = sb("wg_hi_lo", [P, 2, EXPERTS], F32R)
        w1_hi = sb("w1_hi", [P, SLICES * P], F32R)
        w1_lo = sb("w1_lo", [P, SLICES * P], F32R)
        w2_sb = sb("w2_sb", [P, SLICES, D])
        b2_sb = sb("b2_sb", [EXPERTS, D])
        b1_sb = sb("b1_sb", [P, SLICES])
        bq_sb = sb("bq_sb", [P, 1])
        bk_sb = sb("bk_sb", [P, 1])
        rows = sb("rows", [P, 4, D])
        bv_row, bo_row, gamma_row, beta_row = (rows[:, k:k + 1, :].to_broadcast([P, TILES, D]) for k in range(4))
        bg_row = sb("bg_row", [P, 1, EXPERTS])
        expert_no = sb("expert_no", [P, 1, EXPERTS])
        minus_half = sb("minus_half", [P, TILES])

        k_stack = sb("k_stack", [P, HEADS, SEQ], F32R)
        q_stack = [sb(f"q_stack{k}", [P, HEADS, BLOCK], F32R) for k in range(2)]
        v_sb = sb("v_sb", [P, CHUNKS, D])
        one_column = sb("one_column", [P, 2, DH])
        probs = sb("probs", [P, E_RING, 2, BLOCK])
        ctx_part = sb("ctx_part", [P, PART_RING, SQUARES, DH])
        z_part = sb("z_part", [P, SQUARES, DH])
        z_inv = sb("z_inv", [P, 2, SQUARES, 1])
        ctx_sum = sb("ctx_sum", [P, 2, SQUARES, DH])

        x_in = sb("x_in", [P, TILES, D])
        xn = sb("xn", [P, TILES, D])
        xnbo = sb("xnbo", [P, TILES, D])
        xnT_hi = sb("xnT_hi", [P, BLOCK], F32R)
        xnT_lo = sb("xnT_lo", [P, BLOCK], F32R)
        q_hi = sb("q_hi", [P, BLOCK], F32R)
        q_lo = sb("q_lo", [P, BLOCK], F32R)
        k_hi = [sb(f"k_hi{k}", [P, BLOCK], F32R) for k in range(2)]
        k_lo = [sb(f"k_lo{k}", [P, BLOCK], F32R) for k in range(2)]
        v_new = [sb(f"v_new{k}", [P, HALF, D]) for k in range(2)]

        ctxT = sb("ctxT", [P, BLOCK])
        ctxT_hi = sb("ctxT_hi", [P, BLOCK], F32R)
        ctxT_lo = sb("ctxT_lo", [P, BLOCK], F32R)
        x_post = sb("x_post", [P, TILES, D])
        xnbo_post = sb("xnbo_post", [P, TILES, D])
        res = sb("res", [P, TILES, D])
        x2 = sb("x2", [P, TILES, D])
        xn2 = sb("xn2", [P, TILES, D])
        xn2T_hi = sb("xn2T_hi", [P, BLOCK], F32R)
        xn2T_lo = sb("xn2T_lo", [P, BLOCK], F32R)

        gates = sb("gates", [P, TILES, EXPERTS])
        best = sb("best", [P, TILES, 8])
        best_at = sb("best_at", [P, TILES, 8], U32)
        is_second = sb("is_second", [P, TILES, EXPERTS])
        gate_lo = sb("gate_lo", [P, TILES, EXPERTS])
        chosen = sb("chosen", [P, 2, TILES, EXPERTS])
        chosenT = sb("chosenT", [EXPERTS, BLOCK])
        hidden = sb("hidden", [P, BURST, BLOCK])
        y_part = sb("y_part", [P, 2, TILES, D])
        y_sum = sb("y_sum", [P, 2, TILES, D])
        primed = sb("primed", [P, 1])

        def bank(name):
            return ctx.enter_context(nc.psum_tensor(name, [P, BLOCK], F32))

        scores_ps = [bank(f"scores_ps{k}") for k in range(2)]
        ctx_ps = bank("ctx_ps")
        z_ps = bank("z_ps")
        y_ps = bank("y_ps")
        shared_ps = bank("shared_ps")
        hidden_ps = [bank("hidden_ps0"), bank("hidden_ps1"), shared_ps]
        expert_ps = [hidden_ps[0], hidden_ps[1], y_ps]

        proj_loaded = sem("proj_loaded")
        rows_loaded = sem("rows_loaded")
        experts_loaded = sem("experts_loaded")
        adj_loaded = sem("adj_loaded")
        zeroed = sem("zeroed")
        passed = sem("passed")
        pool_consts = sem("pool_consts")
        split_hi = sem("split_hi")
        weights_split = sem("weights_split")
        w1_rounded = sem("w1_rounded")
        w1_split = sem("w1_split")
        top_raw = sem("top_raw")
        top_ready = sem("top_ready")

        score_ready = sem("score_ready")
        exp_done = sem("exp_done")
        probs_ready = sem("probs_ready")
        ctx_ready = sem("ctx_ready")
        ctx_turned = sem("ctx_turned")
        z_turned = sem("z_turned")
        z_inverted = sem("z_inverted")
        ctx_scaled = sem("ctx_scaled")
        ctx_added = sem("ctx_added")
        ctxT_ready = sem("ctxT_ready")
        ctxT_split = sem("ctxT_split")

        shared_filled = sem("shared_filled")
        shared_drained = sem("shared_drained")
        hi_ready = {n: sem(f"hi_ready_{n}") for n in ("xnT", "q", "k", "ctxT", "x2T")}

        x_loaded = sem("x_loaded")
        post_loaded = sem2("post_loaded")
        xnbo_stored = sem2("xnbo_stored")
        q_saved = sem("q_saved")
        k_saved = sem("k_saved")
        q_copied = sem("q_copied")
        k_copied = sem2("k_copied")
        v_copied = sem2("v_copied")
        y_stored = sem2("y_stored")

        ln = {}
        for n in ("first", "second", "third"):
            ln[n] = dict(stats=sb(f"ln_stats_{n}", [P, TILES, 6]), mv=sb(f"ln_mv_{n}", [P, TILES, 2]),
                         rstd=sb(f"ln_rstd_{n}", [P, TILES]), s_stats=sem(f"ln_stats_ready_{n}"),
                         s_mv=sem(f"ln_mv_ready_{n}"), s_eps=sem(f"ln_eps_added_{n}"),
                         s_rstd=sem(f"ln_rstd_ready_{n}"), s_out=sem(f"ln_out_ready_{n}"))

        xnbo_ready = sem("xnbo_ready")
        x_beta_ready = sem("x_beta_ready")
        res_scaled = sem("res_scaled")
        x2_ready = sem("x2_ready")

        gate_lo_ready = sem("gate_lo_ready")
        best_ready = sem("best_ready")
        best_at_ready = sem("best_at_ready")
        ranks_ready = sem("ranks_ready")
        chosen_ready = sem("chosen_ready")

        hidden_pre = sem("hidden_pre")
        hidden_ready = sem("hidden_ready")
        hidden_used = sem("hidden_used")
        table_primed = sem("table_primed")
        y_masked = sem("y_masked")
        y_added = sem("y_added")

        def need_apart(eng, sem_, value):
            need(eng, sem_, value)
            eng.sem_inc(passed, 1)

        proj_stage = probs[:, 0, 0, :]
        w1_stage = hidden[:].rearrange("p a b -> p (a b)")[:, 0:SLICES * P]
        wg_stage = hidden[:, BURST - 1, 0:EXPERTS]

        W_Q, W_K, W_V, W_O = range(4)
        KEYS = HALF * P

        block = ctx.enter_context(nc.Block())

        @block.sync
        def _(sp):
            def row(ap, n):
                return ap.rearrange("(a n) -> a n", a=1).to_broadcast([P, n])

            def column(ap):
                return ap.rearrange("(p a) -> p a", a=1)

            def by_head(part):
                return part.rearrange("(h r) n -> r h n", r=DH)

            def load_x(v):
                sp.dma_start(x_in[:], x_blocks[v]).then_inc(x_loaded, 16)

            load_x(0)
            for k, w in enumerate((wqT, wkT, wvT, woT)):
                sp.dma_start(proj_stage[:, k * D:(k + 1) * D], w).then_inc(proj_loaded, 16)
            for dst, src in ((bq_sb[:], column(bq)), (bk_sb[:], column(bk))):
                sp.dma_start(dst, src).then_inc(proj_loaded, 16)
            for k, b in enumerate((bv, bo, gamma, beta)):
                sp.dma_start(rows[:, k, :], row(b, D)).then_inc(rows_loaded, 16)
            for dst, src in ((w1_stage.rearrange("p (e h) -> p e h", e=EXPERTS), w1.rearrange("e d h -> d e h")),
                             (wg_stage, wg), (bg_row[:, 0, :], row(bg, EXPERTS)),
                             (b1_sb[:], b1T), (b2_sb[:], b2),
                             (w2_sb[:].rearrange("p (e k) d -> p e k d", e=EXPERTS),
                              w2.rearrange("e (k p) d -> p e k d", p=P))):
                sp.dma_start(dst, src).then_inc(experts_loaded, 16)

            def load_mask(chunks):
                for c in chunks:
                    sp.dma_start(top_i[:, c, :], adjT[c * P:(c + 1) * P, :]).then_inc(adj_loaded, 16)

            def copy_q(u, d, in_use):
                v = u.par(d)
                need_apart(sp, shared_drained, u.shared("q", back=2 - d))
                need(sp, score_ready, u.lin(2 * STEPS, 0) if in_use else 0)
                for k, part in enumerate((q_hi, q_lo)):
                    sp.dma_start(q_scratch[k], part[:].bitcast(F32)).then_inc(q_saved, 16)
                sp.wait_ge(q_saved, u.lin(32, 32 * (d + 1)))
                for g, k in enumerate((0, 0, 1, 1)):
                    sp.dma_start(q_stack[v][DH * g:DH * (g + 1), :, :].bitcast(F32),
                                 by_head(q_scratch[k])).then_inc(q_copied, 16)

            def copy_kv(u, d, in_use):
                v = u.par(d)
                step = 0 if v else HALF * 2
                need_apart(sp, shared_drained, u.shared("k", back=2 - d))
                need(sp, score_ready, u.lin(2 * STEPS, 2 * step) if in_use else 0)
                for k, part in enumerate((k_hi, k_lo)):
                    sp.dma_start(k_scratch[k], part[v][:].bitcast(F32)).then_inc(k_saved, 16)
                sp.wait_ge(k_saved, u.lin(32, 32 * (d + 1)))
                for g, k in enumerate((0, 1, 0, 1)):
                    sp.dma_start(k_stack[DH * g:DH * (g + 1), :, KEYS * v:KEYS * (v + 1)].bitcast(F32),
                                 by_head(k_scratch[k])).then_inc(k_copied[v], 16)
                need_apart(sp, shared_drained, u.shared("v", back=2 - d))
                need(sp, ctx_ready, u.lin(CHUNKS, step // 2) if in_use else 0)
                sp.dma_start(v_sb[:, HALF * v:HALF * (v + 1), :], v_new[v][:]).then_inc(v_copied[v], 16)

            def body(u):
                copy = u.has(1) and (u.loop or u.u >= 1)
                if copy:
                    copy_q(u, 1, True)
                    if u.par(1):
                        copy_kv(u, 1, True)
                if u.has(3) and (u.loop or u.u not in (FIRST, -1)):
                    need(sp, ln["first"]["s_out"], u.lin(1, 3))
                    load_x(u.lin(1, 3))
                if not u.loop and u.u in (-2, -1):
                    load_mask(range(HALF) if u.u == -2 else range(HALF, CHUNKS))
                    copy_kv(u, 2, False)
                    if u.u == -2:
                        sp.wait_ge(ln["first"]["s_out"], 2)
                        load_x(2)
                    copy_q(u, 2, False)
                if u.has(-1):
                    need(sp, x2_ready, u.lin(1, -1))
                    need(sp, xnbo_stored[u.par(-1)], u.twos(-1, 16))
                    sp.dma_start(x_post[:], x_blocks[u.lin(1, -1)]).then_inc(post_loaded[u.par(-1)], 16)
                    sp.dma_start(xnbo_post[:], scratch[u.lin(1, -1)]).then_inc(post_loaded[u.par(-1)], 16)
                if copy and not u.par(1):
                    copy_kv(u, 1, True)
                if u.has(-3):
                    need(sp, y_added, u.lin(EXPERTS, -2 * EXPERTS))
                    sp.dma_start(out_blocks[u.lin(1, -3)], y_sum[:, u.par(-3), :, :]).then_inc(y_stored[u.par(-3)], 16)
                if u.has(3):
                    need(sp, xnbo_ready, u.lin(1, 4))
                    sp.dma_start(scratch[u.lin(1, 3)], xnbo[:]).then_inc(xnbo_stored[u.par(3)], 16)

            rounds(sp, body)
            for k in range(2):
                sp.wait_ge(y_stored[k], 16 * BLOCKS // 2)
                sp.wait_ge(xnbo_stored[k], 16 * BLOCKS // 2)

        @block.tensor
        def _(pe):
            def fill(name, u, emit):
                need(pe, shared_drained, u.shared(name) + (-1))
                if name in ("xnT", "x2T") and u.has(-3):
                    need(pe, hidden_ready, u.lin(SLICES, -2 * SLICES))
                if name == "b2":
                    need(pe, hidden_ready, u.lin(SLICES, BURST - 2 * SLICES))
                emit().then_inc(shared_filled, 1)

            def transposes(src):
                for t in range(TILES):
                    last = pe.transpose(shared_ps[:, t * P:(t + 1) * P], src[:, t, :], ident[:])
                return last

            def three(dst, l_hi, l_lo, r_hi, r_lo):
                pe.matmul(dst, l_hi, r_hi, start=True, stop=False)
                pe.matmul(dst, l_hi, r_lo, start=False, stop=False)
                return pe.matmul(dst, l_lo, r_hi, start=False, stop=True)

            def shared_use(name, u):
                if name == "xnT":
                    need(pe, ln["first"]["s_out"], u.lin(1, 3))
                    fill(name, u, lambda: transposes(xn))
                elif name in ("q", "k"):
                    w = W_Q if name == "q" else W_K
                    if name == "k":
                        need(pe, weights_split, 1)
                    fill(name, u, lambda: three(shared_ps[:], w_hi[:, w, :], w_lo[:, w, :], xnT_hi[:], xnT_lo[:]))
                elif name == "v":
                    def emit():
                        for t in range(TILES):
                            cols = slice(t * P, (t + 1) * P)
                            last = three(shared_ps[:, cols], xnT_hi[:, cols], xnT_lo[:, cols],
                                         w_hi[:, W_V, :], w_lo[:, W_V, :])
                        return last
                    fill(name, u, emit)
                elif name == "proj":
                    need(pe, ctxT_split, u.lin(1, 0))

                    def emit():
                        for t in range(TILES):
                            cols = slice(t * P, (t + 1) * P)
                            last = three(shared_ps[:, cols], ctxT_hi[:, cols], ctxT_lo[:, cols],
                                         w_hi[:, W_O, :], w_lo[:, W_O, :])
                        return last
                    fill(name, u, emit)
                elif name == "x2T":
                    need(pe, ln["third"]["s_out"], u.lin(1, -1))
                    fill(name, u, lambda: transposes(xn2))
                elif name == "gate":
                    def emit():
                        for t in range(TILES):
                            cols = slice(t * P, (t + 1) * P)
                            dst = shared_ps[:, 2 * t * EXPERTS:2 * (t + 1) * EXPERTS]
                            both = wg_hi_lo[:].rearrange("p a e -> p (a e)")
                            pe.matmul(dst, xn2T_hi[:, cols], both, start=True, stop=False)
                            last = pe.matmul(dst, xn2T_lo[:, cols], both, start=False, stop=True)
                        return last
                    fill(name, u, emit)
                elif name == "maskT":
                    need(pe, chosen_ready, u.lin(1, -1))

                    def emit():
                        for t in range(TILES):
                            last = pe.transpose(shared_ps[0:EXPERTS, t * P:(t + 1) * P],
                                                chosen[:, u.par(-2), t, :], ident[:])
                        return last
                    fill(name, u, emit)
                elif name == "b2":
                    def emit():
                        for t in range(TILES):
                            last = pe.matmul(shared_ps[:, t * P:(t + 1) * P], chosenT[:, t * P:(t + 1) * P],
                                             b2_sb[:], start=True, stop=True)
                        return last
                    fill(name, u, emit)

            def scores(u, s, hh):
                h, j = 2 * (s % 2) + hh, s // 2
                if hh == 0 and s == 0:
                    pe.wait_ge(q_copied, u.lin(64, 64))
                    if u.par() == 0:
                        pe.wait_ge(k_copied[0], u.twos(0, 64))
                if hh == 0 and s == 2 * HALF and u.par() == 0:
                    pe.wait_ge(k_copied[1], u.twos(1, 64))
                need(pe, exp_done, u.lin(2 * STEPS, 2 * s - 1 + hh))
                pe.matmul(scores_ps[hh][:], k_stack[:, h, j * P:(j + 1) * P], q_stack[u.par()][:, h, :],
                          start=True, stop=True).then_inc(score_ready, 1)

            def context(u, rnd, j):
                if j == 0 and u.par(rnd) == 0:
                    pe.wait_ge(v_copied[0], u.twos(rnd, 16))
                if j == HALF and u.par(rnd) == 0:
                    pe.wait_ge(v_copied[1], u.twos(rnd + 1, 16))
                need(pe, probs_ready, u.lin(STEPS, STEPS * rnd + 2 * j + 2))
                need(pe, ctx_turned, u.lin(CHUNKS, CHUNKS * rnd + j))
                heads = [(slice(DH * h, DH * (h + 1)), probs[:, (2 * j + h // 2) % E_RING, h % 2, :])
                         for h in range(HEADS)]
                for rows_of, e in heads:
                    pe.matmul(ctx_ps[rows_of, :], v_sb[:, j, rows_of], e, start=True, stop=True)
                if j % 2 == 0:
                    need(pe, z_turned, u.lin(CHUNKS // 2, (CHUNKS * rnd + j) // 2))
                for rows_of, e in heads:
                    last = pe.matmul(z_ps[rows_of, :], one_column[:, j % 2, :], e, start=j % 2 == 0, stop=j % 2 == 1,
                                     skip_group_check=True)
                last.then_inc(ctx_ready, 1)

            def first_products(u, k0):
                if not u.loop and u.u == 2 and k0 == 0:
                    pe.wait_ge(w1_split, 4)
                for k in range(BURST):
                    if BURST_BEFORE[k] is not None:
                        need(pe, hidden_ready, u.lin(SLICES, k0 + BURST_BEFORE[k] + 1 - 2 * SLICES))
                    elif BURST_BANK[k] == 2:
                        need(pe, shared_drained, u.upto(BURST - 1 if k0 == 0 else STEPS - 1))
                    else:
                        need(pe, y_masked, u.lin(EXPERTS, k0 // 2 - BURST_BANK[k] - 1 - 2 * EXPERTS))
                    cols = slice((k0 + k) * P, (k0 + k + 1) * P)
                    three(hidden_ps[BURST_BANK[k]][:], w1_hi[:, cols], w1_lo[:, cols], xn2T_hi[:], xn2T_lo[:])\
                        .then_inc(hidden_pre, 1)

            def second_product(u, k, back):
                need(pe, hidden_ready, u.lin(SLICES, k + 1 - back * SLICES))
                e = k // 2
                ps = expert_ps[Y_BANK[e]]
                if k % 2 == 0 and e % 4 >= 2:
                    need(pe, y_masked, u.lin(EXPERTS, (e - 1 if e % 4 == 2 else e - 3) - back * EXPERTS))
                elif k % 2 == 0:
                    last = max(n for n in range(BURST) if BURST_BANK[n] == Y_BANK[e])
                    need(pe, hidden_ready, u.lin(SLICES, k // BURST * BURST + last + 1 - back * SLICES))
                for t in range(TILES):
                    last = pe.matmul(ps[:, t * P:(t + 1) * P], hidden[:, k % BURST, t * P:(t + 1) * P],
                                     w2_sb[:, k, :], start=(k % 2 == 0 and t == 0),
                                     stop=(k % 2 == 1 and t == TILES - 1), skip_group_check=True)
                last.then_inc(hidden_used, 1)

            pe.wait_ge(pool_consts, 2)

            def both_scores(u, s):
                scores(u, s, 0)
                scores(u, s, 1)

            def second(u, s):
                if s < BURST and u.has(-3):
                    second_product(u, BURST + s, 3)
                if s >= BURST and u.has(-2):
                    second_product(u, s - BURST, 2)

            def before_burst(u, s):
                return s in (BURST - 1, STEPS - 1) and u.has(-2)

            def body(u):
                for s in range(STEPS):
                    due = u.chunk(s, CONTEXT_LAG)
                    early = u.scored_early(s)
                    if early and u.has_pair(s, 1):
                        both_scores(u, s + 1)
                    if u.has_pair(s) and not early and not u.scored_early(s - 1):
                        both_scores(u, s)
                    if due is not None:
                        context(u, *due)
                    if s % 2 == 0:
                        second(u, s)
                    if before_burst(u, s):
                        of, at = (u, BURST) if s < BURST else (u.next(), 0)
                        if of.has_pair(at):
                            both_scores(of, at)
                    for at, name, d in SHARED:
                        if at == s and u.has(d):
                            shared_use(name, u)
                    if s % 2 == 1:
                        second(u, s)
                    if before_burst(u, s):
                        first_products(u, 0 if s < BURST else BURST)

            rounds(pe, body)

        @block.scalar
        def _(act):
            act.wait_ge(proj_loaded, 16 * 6)

            def hi_part(u, name, dst, free, bias=None):
                need(act, shared_filled, u.shared(name))
                for s_, v_ in free:
                    need(act, s_, v_)
                if bias is None:
                    ins = nc.scalar.activation(dst, shared_ps[:], ACT.Copy)
                else:
                    ins = nc.scalar.activation(dst, shared_ps[:], ACT.Identity, bias=bias)
                ins.then_inc(hi_ready[name], 1)

            def gelu(u, k0):
                for k in range(k0, k0 + BURST):
                    need(act, hidden_pre, u.lin(SLICES, k + 1 - 2 * SLICES))
                    need(act, hidden_used, u.lin(SLICES, k + 1 - BURST - 2 * SLICES))
                    nc.scalar.activation(hidden[:, k % BURST, :], hidden_ps[BURST_BANK[k % BURST]][:], ACT.Gelu,
                                         bias=b1_sb[:, k:k + 1]).then_inc(hidden_ready, 1)

            def prime_gelu(u, k0):
                n = u.lin(2, (1 if k0 == 0 else 2) - 4)
                need(act, table_primed, n - 1 if isinstance(n, int) else n + (-1))
                nc.scalar.activation(primed[:], b1_sb[:, 0:1], ACT.Gelu).then_inc(table_primed, 1)

            def mask_expert(u, e, back):
                need(act, hidden_used, u.lin(SLICES, 2 * e + 2 - back * SLICES))
                need(act, y_added, u.lin(EXPERTS, e - 1 - back * EXPERTS))
                need(act, chosen_ready, u.lin(1, 1 - back))
                for t in range(TILES):
                    last = nc.scalar.activation(y_part[:, e % 2, t, :],
                                                expert_ps[Y_BANK[e]][:, t * P:(t + 1) * P], ACT.Copy,
                                                scale=chosen[:, u.par(-back), t, e:e + 1])
                last.then_inc(y_masked, 1)

            def exponentials(u, s):
                if not u.loop and u.u == s == 0:
                    act.wait_ge(weights_split, 1)
                for hh in range(2):
                    need(act, score_ready, u.lin(2 * STEPS, 2 * s + hh + 1))
                    if hh == 0:
                        need(act, ctx_ready, u.lin(CHUNKS, (s - E_RING) // 2 + 1))
                    nc.scalar.activation(probs[:, s % E_RING, hh, :], scores_ps[hh][:], ACT.Exp,
                                         scale=SCORE_SCALE).then_inc(exp_done, 1)

            def body(u):
                for s in range(STEPS):
                    if u.has_pair(s) and not u.scored_early(s):
                        exponentials(u, s)
                    if s % 2 == 0 and s <= 8 and u.has(-3):
                        mask_expert(u, 3 + s // 2, 3)
                    if s % 2 == 0 and s >= 10 and u.has(-2):
                        mask_expert(u, (s - 10) // 2, 2)
                    if not u.loop and u.u == 1 and s == 0:
                        act.wait_ge(experts_loaded, 16 * 6)
                    if s in (BURST - 1, STEPS - 1) and u.has(-2):
                        of, at = (u, BURST) if s < BURST else (u.next(), 0)
                        if of.has_pair(at):
                            exponentials(of, at)
                        prime_gelu(u, 0 if s < BURST else BURST)
                    if s == 5 and u.has(-1):
                        if u.has(-2):
                            need(act, shared_filled, u.shared("proj", back=1))
                        need(act, ctxT_ready, u.lin(1, 0))
                        nc.scalar.activation(ctxT_hi[:], ctxT[:], ACT.Copy).then_inc(hi_ready["ctxT"], 1)
                    for at, name, d in SHARED:
                        if at != s or not u.has(d):
                            continue
                        b = u.par(d)
                        if name == "xnT":
                            hi_part(u, name, xnT_hi[:], [(shared_filled, u.shared("q", back=1) if u.has(1) else 0)])
                        elif name == "q":
                            hi_part(u, name, q_hi[:], [(q_copied, u.lin(64, 64 * d))], bq_sb[:, 0:1])
                        elif name == "k":
                            hi_part(u, name, k_hi[b][:], [(k_copied[b], u.twos(d - 2, 64))], bk_sb[:, 0:1])
                        elif name == "maskT":
                            need(act, shared_filled, u.shared(name))
                            nc.scalar.activation(chosenT[:], shared_ps[0:EXPERTS, :], ACT.Copy)\
                                .then_inc(shared_drained, 1)
                        elif name == "x2T":
                            hi_part(u, name, xn2T_hi[:], [(hidden_pre, u.lin(SLICES, -2 * SLICES))])
                    if s in (BURST - 1, STEPS - 1) and u.has(-2):
                        gelu(u, 0 if s < BURST else BURST)

            rounds(act, body)

        @block.vector
        def _(dve):
            def filled(u, name):
                need(dve, shared_filled, u.shared(name))

            def lo_part(u, name, dst, hi, bias=None):
                need(dve, hi_ready[name], u.lin(1, OFFSET[name] + 1))
                if bias is None:
                    ins = dve.tensor_tensor(dst, shared_ps[:], hi.bitcast(F32), ALU.subtract)
                else:
                    ins = dve.scalar_tensor_tensor(out=dst, in0=shared_ps[:], scalar=bias, in1=hi.bitcast(F32),
                                                   op0=ALU.add, op1=ALU.subtract)
                ins.then_inc(shared_drained, 1)

            def statistics(l, src, count):
                for t in range(TILES):
                    last = dve.bn_stats(l["stats"][:, t, :], src[:, t, :])
                last.then_inc(l["s_stats"], 1)
                need_apart(dve, l["s_stats"], count)
                for t in range(TILES):
                    last = dve.bn_aggr(l["mv"][:, t, :], l["stats"][:, t, :])
                last.then_inc(l["s_mv"], 1)

            def normalise(l, dst, src, count):
                dve.wait_ge(l["s_rstd"], count)
                for t in range(TILES):
                    last = dve.tensor_scalar(dst[:, t, :], src[:, t, :], l["mv"][:, t, 0:1], l["rstd"][:, t:t + 1],
                                             ALU.subtract, ALU.mult)
                last.then_inc(l["s_out"], 1)


            def split(n, hi, lo, src):
                dve.tensor_copy(hi, src).then_inc(split_hi, 1)
                dve.wait_ge(split_hi, n)
                dve.tensor_tensor(lo, src, hi.bitcast(F32), ALU.subtract).then_inc(weights_split, 1)

            def mask_chunk(j):
                dve.wait_ge(adj_loaded, 16 * (j // HALF + 1) * HALF)
                dve.tensor_scalar(top[:, j, :], top_i[:, j, :], 0.0, P_HIGH, ALU.not_equal, ALU.mult)\
                    .then_inc(top_raw, 1)
                dve.wait_ge(top_raw, j + 1)
                dve.tensor_scalar(top[:, j, :], top[:, j, :], P_LOW, None, ALU.max).then_inc(top_ready, 1)

            def probabilities(u, s):
                back = s - 1
                ps, nb = back % STEPS, u.par(0 if back >= 0 else -1)
                j = ps // 2
                if not u.loop and u.u <= 1:
                    dve.wait_ge(top_ready, j + 1)
                need(dve, exp_done, u.lin(2 * STEPS, 2 * back + 2))
                e = probs[:, ps % E_RING, :, :]
                bound = top[:, j:j + 1, nb * BLOCK:(nb + 1) * BLOCK].to_broadcast([P, 2, BLOCK])
                dve.scalar_tensor_tensor(out=e, in0=e, scalar=P_LOW, in1=bound, op0=ALU.max, op1=ALU.min)\
                    .then_inc(probs_ready, 1)

            def turn(u, rnd, j):
                need(dve, ctx_ready, u.lin(CHUNKS, CHUNKS * rnd + j + 1))
                need(dve, ctx_added, u.lin(CHUNKS - 1, (CHUNKS - 1) * rnd + max(j - PART_RING, 1) if j >= PART_RING else
                                           (CHUNKS - 1) * (rnd - 1) + CHUNKS - PART_RING + j))
                dve.transpose(ctx_part[:, j % PART_RING, :, :].rearrange("p a b -> p (a b)"), ctx_ps[:])\
                    .then_inc(ctx_turned, 1)
                if j % 2 == 1:
                    dve.transpose(z_part[:].rearrange("p a b -> p (a b)"), z_ps[:]).then_inc(z_turned, 1)

            def invert_sums(u, rnd, j):
                need(dve, z_turned, u.lin(CHUNKS // 2, (CHUNKS * rnd + j + 1) // 2))
                need(dve, ctx_scaled, u.lin(CHUNKS // 2, (CHUNKS * rnd + j - 1) // 2))
                dve.reciprocal(z_inv[:].rearrange("p k s a -> p s (k a)"), z_part[:, :, 0:2]).then_inc(z_inverted, 1)

            def drain(u, name):
                ps3 = shared_ps[:].rearrange("p (t d) -> p t d", t=TILES)
                if name == "xnT":
                    lo_part(u, name, xnT_lo[:], xnT_hi[:])
                elif name == "q":
                    lo_part(u, name, q_lo[:], q_hi[:], bq_sb[:, 0:1])
                elif name == "k":
                    b = u.par(2)
                    lo_part(u, name, k_lo[b][:], k_hi[b][:], bk_sb[:, 0:1])
                elif name == "v":
                    b = u.par(2)
                    filled(u, name)
                    need(dve, v_copied[b], u.twos(0, 16))
                    dve.tensor_tensor(v_new[b][:], ps3, bv_row, ALU.add).then_inc(shared_drained, 1)
                elif name == "proj":
                    filled(u, name)
                    need(dve, post_loaded[u.par(-1)], u.twos(-1, 32))
                    need(dve, x2_ready, u.lin(1, -1))
                    dve.tensor_tensor(res[:], ps3, xnbo_post[:], ALU.add).then_inc(shared_drained, 1)
                elif name == "x2T":
                    lo_part(u, name, xn2T_lo[:], xn2T_hi[:])
                elif name == "gate":
                    filled(u, name)
                    n = u.lin(1, -1)
                    g = shared_ps[:, 0:2 * TILES * EXPERTS].rearrange("p (t a e) -> p t a e", a=2, e=EXPERTS)
                    dve.tensor_tensor(gate_lo[:], g[:, :, 1, :], bg_row[:].to_broadcast([P, TILES, EXPERTS]), ALU.add)\
                        .then_inc(gate_lo_ready, 1)
                    need(dve, gate_lo_ready, n)
                    dve.tensor_tensor(gates[:], g[:, :, 0, :], gate_lo[:], ALU.add).then_inc(shared_drained, 1)
                    need_apart(dve, shared_drained, u.shared(name))
                    for t in range(TILES):
                        last = dve.max(best[:, t, :], gates[:, t, :])
                    last.then_inc(best_ready, 1)
                    need_apart(dve, best_ready, n)
                    for t in range(TILES):
                        last = dve.max_index(best_at[:, t, :], best[:, t, :], gates[:, t, :])
                    last.then_inc(best_at_ready, 1)
                    dve.wait_ge(best_at_ready, n)
                    no = expert_no[:].to_broadcast([P, TILES, EXPERTS])
                    one, two = (best_at[:, :, k:k + 1].to_broadcast([P, TILES, EXPERTS]) for k in range(2))
                    c = chosen[:, u.par(-2), :, :]
                    dve.tensor_tensor(c, no, one, ALU.is_equal)
                    dve.tensor_tensor(is_second[:], no, two, ALU.is_equal).then_inc(ranks_ready, 1)
                    dve.wait_ge(ranks_ready, n)
                    dve.tensor_tensor(c, c, is_second[:], ALU.add).then_inc(chosen_ready, 1)
                elif name == "b2":
                    filled(u, name)
                    need(dve, y_stored[u.par(-2)], u.twos(-4, 16))
                    dve.tensor_tensor(y_sum[:, u.par(-2), :, :], ps3, x2[:], ALU.add).then_inc(shared_drained, 1)

            dve.wait_ge(proj_loaded, 16 * 6)
            split(1, w_hi[:].rearrange("p a b -> p (a b)"), w_lo[:].rearrange("p a b -> p (a b)"), proj_stage)
            dve.wait_ge(pool_consts, 2)
            dve.wait_ge(rows_loaded, 16 * 4)

            def body(u):
                for s in range(STEPS):
                    if not u.loop and (u.u, s) == (-2, 6):
                        dve.wait_ge(experts_loaded, 16 * 6)
                        split(2, wg_hi_lo[:, 0, :], wg_hi_lo[:, 1, :], wg_stage)
                    if not u.loop and u.u == -1 and s in (2, 8):
                        for j in ((0, 1) if s == 2 else (2, 3)):
                            mask_chunk(j)
                    if not u.loop and u.u == 0 and s in (4, 5, 6, 7):
                        mask_chunk(s)
                    if u.has_pair(s, -1):
                        probabilities(u, s)
                    for at, name, d in SHARED:
                        if at == s - 1 and u.has(d):
                            drain(u, name)
                        if at == STEPS - 1 and s == 0 and u.has(d - 1):
                            drain(u.previous(), name)
                    due = u.chunk(s, TURN_LAG)
                    if due is not None:
                        turn(u, *due)
                        if due[1] % 2 == 1:
                            invert_sums(u, *due)
                    if s == 4 and u.has(-1):
                        need(dve, ctxT_split, u.lin(1, -1))
                        need(dve, ctx_added, u.lin(CHUNKS - 1, 0))
                        dve.transpose(ctxT[:], ctx_sum[:, u.par(-1), :, :].rearrange("p a b -> p (a b)"))\
                            .then_inc(ctxT_ready, 1)
                    if s == 6 and u.has(-1):
                        need(dve, hi_ready["ctxT"], u.lin(1, 0))
                        dve.tensor_tensor(ctxT_lo[:], ctxT[:], ctxT_hi[:].bitcast(F32), ALU.subtract)\
                            .then_inc(ctxT_split, 1)
                    if not u.loop and (u.u, s) == (1, 14):
                        dve.wait_ge(x2_ready, 1)
                        statistics(ln["third"], x2, 1)
                    if s == 0 and u.has(-2):
                        if u.loop or u.u > 2:
                            need(dve, x2_ready, u.lin(1, -1))
                            statistics(ln["third"], x2, u.lin(1, -1))
                        need(dve, shared_filled, u.shared("x2T", back=1) if u.has(-3) else 0)
                        normalise(ln["third"], xn2, x2, u.lin(1, -1))
                    at = ln_steps(u)
                    if s == at[0] and u.has(-1):
                        dve.wait_ge(shared_drained, u.shared("proj"))
                        statistics(ln["second"], res, u.lin(1, 0))
                    if s == at[1] and u.has(3):
                        need(dve, x_loaded, u.lin(16, 64))
                        statistics(ln["first"], x_in, u.lin(1, 4))
                    if s == at[2] and u.has(-1):
                        normalise(ln["second"], res, res, u.lin(1, 0))
                    if s == at[3] and u.has(3):
                        need(dve, shared_filled, u.shared("xnT") if u.has(2) else 0)
                        need(dve, xnbo_ready, u.lin(1, 3))
                        normalise(ln["first"], xn, x_in, u.lin(1, 4))

            rounds(dve, body)

        @block.gpsimd
        def _(pool):
            nc.gpsimd.memset(ident[:], 0.0).then_inc(zeroed, 1)
            nc.gpsimd.memset(minus_half[:], -0.5)
            nc.gpsimd.memset(one_column[:], 0.0).then_inc(zeroed, 1)
            pool.wait_ge(zeroed, 2)
            for k in range(2):
                nc.gpsimd.memset(one_column[:, k, k:k + 1], 1.0)
            nc.gpsimd.affine_select(out=ident[:], in_=ident[:], compare_op=ALU.not_equal, fill=1.0, base=0,
                                    pattern=[[-1, P]], channel_multiplier=1).then_inc(pool_consts, 1)
            for e in range(EXPERTS):
                last = nc.gpsimd.memset(expert_no[:, :, e:e + 1], float(e))
            last.then_inc(pool_consts, 1)
            pool.wait_ge(rows_loaded, 16 * 4)
            pool.wait_ge(pool_consts, 2)

            def root(l, count):
                need_apart(pool, l["s_mv"], count)
                nc.gpsimd.tensor_scalar(l["rstd"][:], l["mv"][:, :, 1], LN_EPS, None, ALU.add).then_inc(l["s_eps"], 1)
                pool.wait_ge(l["s_eps"], count)
                nc.gpsimd.tensor_tensor(l["rstd"][:], l["rstd"][:], minus_half[:], ALU.pow).then_inc(l["s_rstd"], 1)

            def scale(u, rnd, j):
                need(pool, z_inverted, u.lin(CHUNKS // 2, (CHUNKS * rnd + j + 1) // 2))
                k = j % PART_RING
                parts = ctx_part[:, k - 1:k + 1, :, :]
                nc.gpsimd.tensor_tensor(parts, parts, z_inv[:].to_broadcast([P, 2, SQUARES, DH]), ALU.mult)\
                    .then_inc(ctx_scaled, 1)

            def add_context(u, rnd, j):
                need(pool, ctx_scaled, u.lin(CHUNKS // 2, (CHUNKS * rnd + j // 2 * 2) // 2 + 1))
                dst = ctx_sum[:, u.par(rnd), :, :]
                if j == 1:
                    need(pool, ctxT_ready, u.lin(1, rnd - 1))
                    first = ctx_part[:, 0, :, :]
                else:
                    need(pool, ctx_added, u.lin(CHUNKS - 1, (CHUNKS - 1) * rnd + j - 1))
                    first = dst
                nc.gpsimd.tensor_tensor(dst, first, ctx_part[:, j % PART_RING, :, :], ALU.add).then_inc(ctx_added, 1)

            def add_expert(u, e, back):
                need(pool, y_masked, u.lin(EXPERTS, e + 1 - back * EXPERTS))
                need(pool, y_added, u.lin(EXPERTS, e - back * EXPERTS))
                if e == 0:
                    need(pool, shared_drained, u.shared("b2"))
                dst = y_sum[:, u.par(-back), :, :]
                nc.gpsimd.tensor_tensor(dst, dst, y_part[:, e % 2, :, :], ALU.add).then_inc(y_added, 1)

            def split_w1(k):
                pool.wait_ge(experts_loaded, 16 * 6)
                cols = slice(k * BLOCK, (k + 1) * BLOCK)
                nc.gpsimd.tensor_copy(w1_hi[:, cols], w1_stage[:, cols]).then_inc(w1_rounded, 1)
                pool.wait_ge(w1_rounded, k + 1)
                nc.gpsimd.tensor_tensor(w1_lo[:, cols], w1_stage[:, cols], w1_hi[:, cols].bitcast(F32), ALU.subtract)\
                    .then_inc(w1_split, 1)

            def body(u):
                for s in range(STEPS):
                    if not u.loop and u.u < 0 and u.u >= -2 and s == 12:
                        split_w1(2 * (u.u + 2))
                        split_w1(2 * (u.u + 2) + 1)
                    if not u.loop and (u.u, s) == (1, 14):
                        root(ln["third"], 1)
                    due = u.chunk(s, TURN_LAG)
                    if due is not None and due[1] % 2 == 1:
                        scale(u, *due)
                        if due[1] > 1:
                            add_context(u, due[0], due[1] - 1)
                        add_context(u, *due)
                    if s == 0 and u.has(-2) and (u.loop or u.u > 2):
                        root(ln["third"], u.lin(1, -1))
                    if s == ln_steps(u)[0] and u.has(-1):
                        root(ln["second"], u.lin(1, 0))
                    if s == ln_steps(u)[1] and u.has(3):
                        root(ln["first"], u.lin(1, 4))
                    if s % 2 == 0 and s <= 8 and u.has(-3):
                        add_expert(u, 3 + s // 2, 3)
                    if s % 2 == 0 and s >= 10 and u.has(-2):
                        add_expert(u, (s - 10) // 2, 2)
                    if s == 5 and u.has(-1):
                        need(pool, post_loaded[u.par(-1)], u.twos(-1, 32))
                        nc.gpsimd.tensor_tensor(x_post[:], x_post[:], beta_row, ALU.add).then_inc(x_beta_ready, 1)
                    if s == 11 and u.has(-1):
                        need(pool, ln["second"]["s_out"], u.lin(1, 0))
                        nc.gpsimd.tensor_tensor(res[:], res[:], gamma_row, ALU.mult).then_inc(res_scaled, 1)
                    if s == 12 and u.has(-1):
                        need(pool, res_scaled, u.lin(1, 0))
                        need(pool, x_beta_ready, u.lin(1, 0))
                        if u.has(-2):
                            need(pool, shared_drained, u.shared("b2"))
                        nc.gpsimd.tensor_tensor(x2[:], res[:], x_post[:], ALU.add).then_inc(x2_ready, 1)
                    if s == 13 and u.has(3):
                        need(pool, ln["first"]["s_out"], u.lin(1, 4))
                        need(pool, xnbo_stored[u.par(2)], u.twos(2, 16))
                        nc.gpsimd.tensor_tensor(xnbo[:], xn[:], bo_row, ALU.add).then_inc(xnbo_ready, 1)

            rounds(pool, body)


def kernel(x, adj, L0_gnn_Wq, L0_gnn_bq, L0_gnn_Wk, L0_gnn_bk, L0_gnn_Wv, L0_gnn_bv, L0_gnn_Wo, L0_gnn_bo,
           L0_gnn_gamma, L0_gnn_beta, L0_ffn_Wg, L0_ffn_bg, L0_ffn_W1, L0_ffn_b1, L0_ffn_W2, L0_ffn_b2):
    import concourse.bacc as bacc
    from concourse.bass_utils import run_bass_kernel_spmd

    laid = dict(x=x, adjT=np.asarray(adj).T, wqT=np.asarray(L0_gnn_Wq).T, bq=L0_gnn_bq,
                wkT=np.asarray(L0_gnn_Wk).T, bk=L0_gnn_bk, wvT=np.asarray(L0_gnn_Wv).T, bv=L0_gnn_bv,
                woT=np.asarray(L0_gnn_Wo).T, bo=L0_gnn_bo, gamma=L0_gnn_gamma, beta=L0_gnn_beta,
                wg=L0_ffn_Wg, bg=L0_ffn_bg, w1=L0_ffn_W1,
                b1T=np.asarray(L0_ffn_b1).reshape(SLICES, P).T, w2=L0_ffn_W2, b2=L0_ffn_b2)
    nc = bacc.Bacc("TRN2", target_bir_lowering=False, num_devices=1)
    arrays, args = {}, []
    for name, value in laid.items():
        a = np.ascontiguousarray(value)
        arrays[f"in_{name}"] = a
        args.append(nc.dram_tensor(f"in_{name}", a.shape, mybir.dt.from_np(a.dtype), kind="ExternalInput").ap())
    out = nc.dram_tensor("out", (BATCH, SEQ, D), F32, kind="ExternalOutput").ap()
    graph_transformer_layer(nc, *args, out)
    results = run_bass_kernel_spmd(nc, [arrays], core_ids=[0])
    return results.results[0]["out"]
```
